# Optimizing a Trainium2 kernel written in Bass

```python
import numpy as np
import jax
import jax.numpy as jnp

def _softmax(x, axis=-1):
    return jax.nn.softmax(x, axis=axis)

def _gelu(x):
    return jax.nn.gelu(x, approximate=True)

def _silu(x):
    return jax.nn.silu(x)

def _sigmoid(x):
    return jax.nn.sigmoid(x)

def _layernorm(x, axis=-1, eps=1e-05):
    m = jnp.mean(x, axis=axis, keepdims=True)
    v = jnp.var(x, axis=axis, keepdims=True)
    return (x - m) / jnp.sqrt(v + eps)

def _scatter_add(tgt, idx, src, axis=0):
    return tgt.at[idx].add(src)

def _segment_sum(src, seg, n):
    return jax.ops.segment_sum(src, seg, n)
kernel_name = 'mk_prb_d1_jaxref_r2_cb913a'

def setup_inputs(seed: int=0):
    np.random.seed(seed)
    _w = jnp.asarray

    def _L0_attn_setup():
        import jax, jax.numpy as jnp
        import numpy as np
        D_EMB = 512
        D_ATTN = 512
        NUM_HEADS = 16
        HEAD_DIM = D_ATTN // NUM_HEADS
        SEQ = 1024
        BS = 2
        key = jax.random.key(seed)
        ks = jax.random.split(key, 6)
        s = 1.0 / np.sqrt(D_EMB)
        return {'x': jax.random.normal(ks[0], (BS, SEQ, D_EMB), dtype=jnp.float32), 'W_q': jax.random.uniform(ks[1], (D_ATTN, D_EMB), jnp.float32, -s, s), 'W_k': jax.random.uniform(ks[2], (D_ATTN, D_EMB), jnp.float32, -s, s), 'W_v': jax.random.uniform(ks[3], (D_ATTN, D_EMB), jnp.float32, -s, s), 'W_o': jax.random.uniform(ks[4], (D_ATTN, D_ATTN), jnp.float32, -s, s), 'b_o': jax.random.uniform(ks[5], (D_ATTN,), jnp.float32, -s, s)}
    _L0_attn_in = _L0_attn_setup()

    def _L0_ffn_setup():
        import jax, jax.numpy as jnp
        import numpy as np
        DIM = 512

        def _reference_tuple_inner(x, W_r, W_k, W_v, mu_r, mu_k):
            B, T, C = x.shape
            x_prev = jnp.concatenate([jnp.zeros((B, 1, C), x.dtype), x[:, :-1, :]], axis=1)
            xr = mu_r * x + (1.0 - mu_r) * x_prev
            xk = mu_k * x + (1.0 - mu_k) * x_prev
            r = jax.nn.sigmoid(jnp.einsum('btc,dc->btd', xr, W_r))
            k = jnp.einsum('btc,dc->btd', xk, W_k)
            k_act = jnp.square(jax.nn.relu(k))
            out = r * jnp.einsum('btc,dc->btd', k_act, W_v)
            new_state = x[:, -1, :]
            return (out, new_state)
        key = jax.random.key(seed)
        ks = jax.random.split(key, 6)
        B, T, C = (8, 1024, DIM)
        x = jax.random.normal(ks[0], (B, T, C), dtype=jnp.float32)
        s = 1.0 / np.sqrt(C)
        W_r = jax.random.uniform(ks[1], (C, C), jnp.float32, -s, s)
        W_k = jax.random.uniform(ks[2], (C, C), jnp.float32, -s, s)
        W_v = jax.random.uniform(ks[3], (C, C), jnp.float32, -s, s)
        mu_r = jax.random.uniform(ks[4], (C,), jnp.float32)
        mu_k = jax.random.uniform(ks[5], (C,), jnp.float32)
        return {'x': x, 'W_r': W_r, 'W_k': W_k, 'W_v': W_v, 'mu_r': mu_r, 'mu_k': mu_k}
    _L0_ffn_in = _L0_ffn_setup()
    _d = {'L0_attn_x': _L0_attn_in['x'], 'L0_attn_W_q': _L0_attn_in['W_q'], 'L0_attn_W_k': _L0_attn_in['W_k'], 'L0_attn_W_v': _L0_attn_in['W_v'], 'L0_attn_W_o': _L0_attn_in['W_o'], 'L0_attn_b_o': _L0_attn_in['b_o'], 'L0_ffn_W_r': _L0_ffn_in['W_r'], 'L0_ffn_W_k': _L0_ffn_in['W_k'], 'L0_ffn_W_v': _L0_ffn_in['W_v'], 'L0_ffn_mu_r': _L0_ffn_in['mu_r'], 'L0_ffn_mu_k': _L0_ffn_in['mu_k']}
    _x0 = _d['L0_attn_x']
    _d['L0_attn_x'] = jax.random.normal(jax.random.fold_in(jax.random.key(seed), 1), (4, 2048, 512), dtype=_x0.dtype)
    del _x0
    return _d

def reference(L0_attn_x, L0_attn_W_q, L0_attn_W_k, L0_attn_W_v, L0_attn_W_o, L0_attn_b_o, L0_ffn_W_r, L0_ffn_W_k, L0_ffn_W_v, L0_ffn_mu_r, L0_ffn_mu_k):

    def _L0_attn_ref(x, W_q, W_k, W_v, W_o, b_o):
        import jax, jax.numpy as jnp
        import numpy as np
        D_EMB = 512
        D_ATTN = 512
        NUM_HEADS = 16
        HEAD_DIM = D_ATTN // NUM_HEADS
        SEQ = 1024
        BS = 2
        bs, seq_len, _ = x.shape
        q = jnp.einsum('bse,ae->bsa', x, W_q).reshape(bs, seq_len, NUM_HEADS, HEAD_DIM)
        k = jnp.einsum('bse,ae->bsa', x, W_k).reshape(bs, seq_len, NUM_HEADS, HEAD_DIM)
        v = jnp.einsum('bse,ae->bsa', x, W_v).reshape(bs, seq_len, NUM_HEADS, HEAD_DIM)
        q = q.transpose(0, 2, 1, 3)
        k = k.transpose(0, 2, 1, 3)
        v = v.transpose(0, 2, 1, 3)
        scores = jnp.einsum('bhqd,bhkd->bhqk', q, k)
        causal = jnp.tril(jnp.ones((seq_len, seq_len), dtype=bool))
        scores = jnp.where(causal, scores, -jnp.inf)
        attn = jax.nn.softmax(scores / np.sqrt(HEAD_DIM), axis=-1)
        ctx = jnp.einsum('bhqk,bhkd->bhqd', attn, v)
        ctx = ctx.transpose(0, 2, 1, 3).reshape(bs, seq_len, D_ATTN)
        return jnp.einsum('bsa,oa->bso', ctx, W_o) + b_o

    def _L0_ffn_ref(x, W_r, W_k, W_v, mu_r, mu_k):
        import jax, jax.numpy as jnp
        import numpy as np
        DIM = 512

        def _reference_tuple_inner(x, W_r, W_k, W_v, mu_r, mu_k):
            B, T, C = x.shape
            x_prev = jnp.concatenate([jnp.zeros((B, 1, C), x.dtype), x[:, :-1, :]], axis=1)
            xr = mu_r * x + (1.0 - mu_r) * x_prev
            xk = mu_k * x + (1.0 - mu_k) * x_prev
            r = jax.nn.sigmoid(jnp.einsum('btc,dc->btd', xr, W_r))
            k = jnp.einsum('btc,dc->btd', xk, W_k)
            k_act = jnp.square(jax.nn.relu(k))
            out = r * jnp.einsum('btc,dc->btd', k_act, W_v)
            new_state = x[:, -1, :]
            return (out, new_state)
        return _reference_tuple_inner(x, W_r, W_k, W_v, mu_r, mu_k)[0]
    x = L0_attn_x
    xn = _layernorm(x, axis=-1)
    x = x + _L0_attn_ref(xn, L0_attn_W_q, L0_attn_W_k, L0_attn_W_v, L0_attn_W_o, L0_attn_b_o) + _L0_ffn_ref(xn, L0_ffn_W_r, L0_ffn_W_k, L0_ffn_W_v, L0_ffn_mu_r, L0_ffn_mu_k)
    return x

_drawn_inputs = setup_inputs


def setup_inputs(seed=0):
    import zlib

    import numpy as np

    out = dict(_drawn_inputs(seed))
    spreads = {}
    factors = {'L0_attn_W_q': 6.755, 'L0_attn_W_k': 6.449, 'L0_ffn_W_r': 3.158, 'L0_ffn_mu_r': 6.455}
    for name, (base, spread) in spreads.items():
        noise = np.random.default_rng([zlib.crc32(name.encode()), seed]).standard_normal(out[name].shape)
        drawn = base * np.exp(spread * noise) if base else spread * noise
        out[name] = jnp.asarray(drawn.astype(out[name].dtype))
    for name, factor in factors.items():
        out[name] = (out[name] * factor).astype(out[name].dtype)
    return out
```

```python
from contextlib import ExitStack

import concourse.bass as bass
from concourse import mybir

F32 = mybir.dt.float32
F32R = mybir.dt.float32r
BF16 = mybir.dt.bfloat16
ALU = mybir.AluOpType
ACT = mybir.ActivationFunctionType
AX_X = mybir.AxisListType.X

P = 128
B, T, D = 4, 2048, 512
H, HD = 16, 32
HG = P // HD
G = H // HG
BLK = 512
NB = T // BLK
ET = D // P
TT = BLK // P
QK_ROWS = 3 * HD
SCALE = float(HD) ** -0.5
EPS = 1e-5
MASKED = -1e30

FIRST = 1
DMA_FIRST = 16



def start_counters(eng, counters, dma_counters):
    for c in counters:
        eng.sem_inc(c, FIRST)
    for c in dma_counters:
        eng.sem_inc(c, DMA_FIRST)


def project_and_ffn(nc, x, w_t, b_o, mu_r, mu_k, q_hi, q_lo, k_hi, k_lo, v_all, part):
    NT = 2 * G + 4 * TT
    RING = 6
    Q0, K0, V0, R0, C0, F0 = 0, G, 2 * G, 2 * G + TT, 2 * G + 2 * TT, 2 * G + 3 * TT
    NS = 4
    with ExitStack() as ctx:
        def sb(name, shape, dt=F32):
            return ctx.enter_context(nc.sbuf_tensor(name, shape, dt))

        def sem(name):
            return ctx.enter_context(nc.semaphore(name))

        w_hi = [sb(f"w_hi{n}", [P, ET, D], F32R) for n in range(6)]
        w_lo = [sb(f"w_lo{n}", [P, ET, D], F32R) for n in range(6)]
        xb = [sb(f"x_block{s}", [P, TT, D]) for s in range(2)]
        xn = sb("xn", [P, TT, D])
        xf = sb("xn_t", [P, ET, BLK + 1])
        mix = sb("mix", [P, ET, BLK])
        a_hi = sb("a_hi", [P, ET, BLK], F32R)
        a_lo = sb("a_lo", [P, ET, BLK], F32R)
        b_hi = sb("b_hi", [P, ET, BLK], F32R)
        b_lo = sb("b_lo", [P, ET, BLK], F32R)
        st_hi = [sb(f"st_hi{s}", [P, BLK], F32R) for s in range(NS)]
        st_lo = [sb(f"st_lo{s}", [P, BLK], F32R) for s in range(NS)]
        v_st = [sb(f"v_st{s}", [P, D]) for s in range(2)]
        gate = sb("gate", [P, TT, D])
        relu = [sb(f"relu{s}", [P, BLK]) for s in range(2)]
        f_out = [sb(f"f_out{s}", [P, D]) for s in range(2)]
        bias = sb("bias", [P, D])
        mus = sb("mus", [P, 2, ET])
        ident = sb("ident", [P, P])
        stats = sb("stats", [P, TT, 6])
        mean_var = sb("mean_var", [P, TT, 2])
        var_eps = sb("var_eps", [P, TT])
        sd = sb("sd", [P, TT])
        rstd = sb("rstd", [P, TT])
        ring = [ctx.enter_context(nc.psum_tensor(f"ring{s}", [P, BLK], F32)) for s in range(RING)]
        tps = [ctx.enter_context(nc.psum_tensor(f"tps{s}", [P, BLK], F32)) for s in range(2)]

        w_ld = [sem(f"w_loaded{s}") for s in range(2)]
        w_split_hi = sem("w_split_hi")
        w_split = sem("w_split")
        small_ld = sem("small_loaded")
        x_ld = [sem(f"x_loaded{s}") for s in range(2)]
        ones_set = sem("ones_set")
        ident_set = sem("ident_set")
        stats_done = sem("stats_done")
        aggr_done = sem("aggr_done")
        var_done = sem("var_done")
        sd_done = sem("sd_done")
        rstd_done = sem("rstd_done")
        xn_done = sem("xn_done")
        res_done = sem("residual_done")
        t_done = sem("transposed")
        xf_done = sem("xn_t_ready")
        xhi_done = sem("xn_hi_ready")
        xlo_done = sem("xn_lo_ready")
        col_zero = sem("column0_ready")
        step_done = sem("step_ready")
        mix_done = sem("mix_ready")
        mhi_done = sem("mix_hi_ready")
        mlo_done = sem("mix_lo_ready")
        tile_done = sem("tile_done")
        qk_done = sem("qk_split")
        st_hi_done = sem("stage_hi")
        stored = [sem(f"stage_stored{s}") for s in range(NS)]
        v_done = sem("v_done")
        v_stored = [sem(f"v_stored{s}") for s in range(2)]
        tanh_done = sem("tanh_done")
        gate_done = sem("gate_done")
        relu_done = sem("relu_done")
        sq_done = sem("square_done")
        chi_done = sem("key_hi_ready")
        clo_done = sem("key_lo_ready")
        f_done = sem("f_done")
        part_done = sem("part_done")
        part_stored = [sem(f"part_stored{s}") for s in range(2)]

        LAST_READER = [(qk_done, Q0, 2 * G), (v_done, V0, TT), (tanh_done, R0, TT), (relu_done, C0, TT),
                       (f_done, F0, TT)]

        def wait_ring(eng, n0, m):
            i, blk = n0
            prev = blk * NT + m - RING
            for done, first, count in LAST_READER:
                if prev < 0:
                    eng.wait_ge(done, i * (NB * count) + FIRST)
                elif first <= prev % NT < first + count:
                    eng.wait_ge(done, i * (NB * count) + prev // NT * count + prev % NT - first + 1 + FIRST)

        with nc.Block() as block:
            @block.sync
            def _(sp):
                start_counters(sp, [qk_done, v_done, tanh_done, relu_done, f_done, clo_done, mlo_done],
                               stored + v_stored + part_stored)
                sp.dma_start(xb[0][:], x[0:BLK, :].rearrange("(t p) d -> p t d", p=P)).then_inc(x_ld[0], 16)
                sp.dma_start(bias[:], b_o).then_inc(small_ld, 16)
                sp.dma_start(mus[:, 0, :], mu_r).then_inc(small_ld, 16)
                sp.dma_start(mus[:, 1, :], mu_k).then_inc(small_ld, 16)
                for n in range(6):
                    if n >= 2:
                        sp.wait_ge(w_split, n - 1)
                    sp.dma_start((mix, gate)[n % 2][:], w_t[n].rearrange("(t p) a -> p t a", p=P)
                                 ).then_inc(w_ld[n % 2], 16)
                sp.dma_start(xb[1][:], x[BLK:2 * BLK, :].rearrange("(t p) d -> p t d", p=P)).then_inc(x_ld[1], 16)
                with sp.Fori(0, B) as i:
                    for blk in range(NB):
                        for m in range(2 * G):
                            c = blk * 2 * G + m
                            g = m % G
                            hi, lo = (q_hi, q_lo) if m < K0 else (k_hi, k_lo)
                            rows = bass.ds(i * (G * P) + g * P, P)
                            sp.wait_ge(qk_done, i * (NB * 2 * G) + c + 1 + FIRST)
                            for dst, src in ((hi, st_hi), (lo, st_lo)):
                                sp.dma_start(dst[rows, blk * BLK:(blk + 1) * BLK], src[c % NS][:].bitcast(F32)
                                             ).then_inc(stored[c % NS], 16)
                        for t in range(TT):
                            c = blk * TT + t
                            sp.wait_ge(v_done, i * (NB * TT) + c + 1 + FIRST)
                            dst = v_all[bass.ds(i * (G * T), G * T), :].rearrange("(g t) c -> t g c", g=G)
                            sp.dma_start(dst[c * P:(c + 1) * P, :, :],
                                         v_st[c % 2][:].rearrange("p (g c) -> p g c", g=G)
                                         ).then_inc(v_stored[c % 2], 16)
                        for t in range(TT):
                            c = blk * TT + t
                            sp.wait_ge(part_done, i * (NB * TT) + c + 1)
                            sp.dma_start(part[bass.ds(i * T + c * P, P), :], f_out[c % 2][:]
                                         ).then_inc(part_stored[c % 2], 16)
                        nxt = blk + 2
                        row = i * T + nxt * BLK if nxt < NB else ((i + 1) % B) * T + (nxt - NB) * BLK
                        sp.dma_start(xb[blk % 2][:], x[bass.ds(row, BLK), :].rearrange("(t p) d -> p t d", p=P)
                                     ).then_inc(x_ld[blk % 2], 16)
                for s in range(2):
                    sp.wait_ge(x_ld[s], 16 * (B * NB // 2 + 1))
                for s in range(NS):
                    sp.wait_ge(stored[s], B * NB * 2 * G // NS * 32 + DMA_FIRST)
                for s in range(2):
                    sp.wait_ge(v_stored[s], B * NB * TT // 2 * 16 + DMA_FIRST)
                    sp.wait_ge(part_stored[s], B * NB * TT // 2 * 16 + DMA_FIRST)

            @block.gpsimd
            def _(pool):
                nc.gpsimd.memset(ident[:], 1.0).then_inc(ones_set, 1)
                pool.wait_ge(ones_set, 1)
                nc.gpsimd.affine_select(out=ident[:], in_=ident[:], compare_op=ALU.is_equal, fill=0.0, base=0,
                                        pattern=[[-1, P]], channel_multiplier=1).then_inc(ident_set, 1)
                pool.wait_ge(small_ld, 48)

                def residual(buf, n):
                    pool.wait_ge(xn_done, n)
                    for t in range(TT):
                        nc.gpsimd.tensor_tensor(buf[:, t, :], buf[:, t, :], bias[:], ALU.add).then_inc(res_done, 1)

                residual(xb[0], TT)
                with pool.Fori(0, B) as i:
                    for blk in range(NB):
                        n = i * NB + blk
                        residual(xb[(blk + 1) % 2], (n + 2) * TT)
                        for t in range(TT):
                            c = blk * TT + t
                            pool.wait_ge(f_done, i * (NB * TT) + c + 1 + FIRST)
                            pool.wait_ge(res_done, (n + 1) * TT)
                            nc.gpsimd.tensor_tensor(f_out[c % 2][:], f_out[c % 2][:], xb[blk % 2][:, t, :],
                                                    ALU.add).then_inc(part_done, 1)

            @block.scalar
            def _(act):
                def split_w(n):
                    act.wait_ge(w_ld[n % 2], 16 * (n // 2 + 1))
                    nc.scalar.activation(w_hi[n][:], (mix, gate)[n % 2][:], ACT.Copy).then_inc(w_split_hi, 1)

                def root(n):
                    act.wait_ge(var_done, n)
                    nc.scalar.activation(sd[:], var_eps[:], ACT.Sqrt).then_inc(sd_done, 1)

                def take_transposed(n):
                    def hi(e):
                        act.wait_ge(xf_done, n * ET + e + 1)
                        nc.scalar.activation(a_hi[:, e, :], xf[:, e, 1:BLK + 1], ACT.Copy).then_inc(xhi_done, 1)
                    for e in range(ET):
                        act.wait_ge(t_done, n * ET + e + 1)
                        if e == 0:
                            act.wait_ge(col_zero, n + 1)
                        nc.scalar.activation(xf[:, e, 1:BLK + 1], tps[e % 2][:], ACT.Copy).then_inc(xf_done, 1)
                        if e >= 1:
                            hi(e - 1)
                    hi(ET - 1)

                root(1)
                for n in range(6):
                    split_w(n)
                take_transposed(0)
                with act.Fori(0, B) as i:
                    for blk in range(NB):
                        n = i * NB + blk
                        tile0 = i * (NB * NT) + blk * NT
                        for m in range(2 * G):
                            c = blk * 2 * G + m
                            act.wait_ge(tile_done, tile0 + m + 1)
                            use = c // NS
                            act.wait_ge(stored[c % NS], i * (NB * 2 * G // NS * 32) + 32 * use + DMA_FIRST)
                            nc.scalar.activation(st_hi[c % NS][:], ring[(blk * NT + m) % RING][:], ACT.Copy
                                                 ).then_inc(st_hi_done, 1)
                            if m == 3:
                                act.wait_ge(mix_done, (n * 2 + 1) * ET)
                                nc.scalar.activation(b_hi[:], mix[:], ACT.Copy).then_inc(mhi_done, 1)
                        for t in range(TT):
                            c = blk * TT + t
                            act.wait_ge(tile_done, tile0 + V0 + t + 1)
                            act.wait_ge(v_stored[c % 2], i * (NB * TT // 2 * 16) + 16 * (c // 2) + DMA_FIRST)
                            nc.scalar.activation(v_st[c % 2][:], ring[(blk * NT + V0 + t) % RING][:], ACT.Copy)\
                                .then_inc(v_done, 1)
                        act.wait_ge(mix_done, (n * 2 + 2) * ET)
                        nc.scalar.activation(a_hi[:], mix[:], ACT.Copy).then_inc(mhi_done, 1)
                        root(n + 2)
                        for t in range(TT):
                            act.wait_ge(tile_done, tile0 + R0 + t + 1)
                            act.wait_ge(f_done, n * TT + FIRST)
                            nc.scalar.activation(gate[:, t, :], ring[(blk * NT + R0 + t) % RING][:], ACT.Tanh,
                                                 scale=0.5).then_inc(tanh_done, 1)

                        def key_hi(t):
                            act.wait_ge(sq_done, n * TT + t + 1)
                            nc.scalar.activation(b_hi[:, t, :], relu[t % 2][:], ACT.Copy).then_inc(chi_done, 1)
                        for t in range(TT):
                            act.wait_ge(tile_done, tile0 + C0 + t + 1)
                            if t >= 2:
                                act.wait_ge(clo_done, n * TT + t - 1 + FIRST)
                            else:
                                act.wait_ge(clo_done, n * TT + FIRST)
                            nc.scalar.activation(relu[t % 2][:], ring[(blk * NT + C0 + t) % RING][:], ACT.Relu)\
                                .then_inc(relu_done, 1)
                            if t >= 1:
                                key_hi(t - 1)
                        key_hi(TT - 1)
                        take_transposed(n + 1)

            @block.vector
            def _(dve):
                def split_w(n):
                    dve.wait_ge(w_split_hi, n + 1)
                    nc.vector.tensor_tensor(w_lo[n][:], (mix, gate)[n % 2][:], w_hi[n][:].bitcast(F32),
                                            ALU.subtract).then_inc(w_split, 1)

                def moments(buf, s, loads, n):
                    dve.wait_ge(x_ld[s], loads)
                    for t in range(TT):
                        nc.vector.bn_stats(stats[:, t, :], buf[:, t, :]).then_inc(stats_done, 1)
                    for t in range(TT):
                        dve.wait_ge(stats_done, n * TT + t + 1)
                        dve.nop(nofuse=True)
                        nc.vector.bn_aggr(mean_var[:, t, :], stats[:, t, :]).then_inc(aggr_done, 1)
                    dve.wait_ge(aggr_done, (n + 1) * TT)
                    nc.vector.tensor_scalar(var_eps[:], mean_var[:, :, 1], EPS, None, ALU.add).then_inc(var_done, 1)

                def normalise(buf, n):
                    dve.wait_ge(sd_done, n + 1)
                    nc.vector.reciprocal(rstd[:], sd[:]).then_inc(rstd_done, 1)
                    dve.wait_ge(rstd_done, n + 1)
                    for t in range(TT):
                        nc.vector.tensor_scalar(xn[:, t, :], buf[:, t, :], mean_var[:, t, 0:1], rstd[:, t:t + 1],
                                                ALU.subtract, ALU.mult).then_inc(xn_done, 1)

                def split_xn(n):
                    for e in range(ET):
                        dve.wait_ge(xhi_done, n * ET + e + 1)
                        nc.vector.tensor_tensor(a_lo[:, e, :], xf[:, e, 1:BLK + 1], a_hi[:, e, :].bitcast(F32),
                                                ALU.subtract).then_inc(xlo_done, 1)

                nc.vector.memset(xf[:, :, 0], 0.0).then_inc(col_zero, 1)
                moments(xb[0], 0, 16, 0)
                normalise(xb[0], 0)
                for n in range(6):
                    split_w(n)
                split_xn(0)
                dve.wait_ge(small_ld, 48)
                dve.wait_ge(col_zero, 1)
                with dve.Fori(0, B) as i:
                    for blk in range(NB):
                        n = i * NB + blk
                        tile0 = i * (NB * NT) + blk * NT

                        def split_tile(m):
                            c = blk * 2 * G + m
                            dve.wait_ge(st_hi_done, i * (NB * 2 * G) + c + 1)
                            nc.vector.tensor_tensor(st_lo[c % NS][:], ring[(blk * NT + m) % RING][:],
                                                    st_hi[c % NS][:].bitcast(F32), ALU.subtract).then_inc(qk_done, 1)

                        def mixed(which):
                            dve.wait_ge(step_done, n + 1)
                            for e in range(ET):
                                nc.vector.scalar_tensor_tensor(
                                    out=mix[:, e, :], in0=xn[:, e, :], scalar=mus[:, which, e:e + 1],
                                    in1=xf[:, e, 0:BLK], op0=ALU.mult, op1=ALU.add).then_inc(mix_done, 1)

                        def mix_lo(which, dst, hi):
                            dve.wait_ge(mhi_done, n * 2 + which + 1)
                            nc.vector.tensor_tensor(dst[:], mix[:], hi[:].bitcast(F32), ALU.subtract)\
                                .then_inc(mlo_done, 1)

                        split_tile(0)
                        dve.wait_ge(xf_done, (n + 1) * ET)
                        nc.vector.tensor_tensor(xn[:], xf[:, :, 1:BLK + 1], xf[:, :, 0:BLK], ALU.subtract)\
                            .then_inc(step_done, 1)
                        split_tile(1)
                        if blk == 0:
                            dve.wait_ge(mlo_done, n * 2 + FIRST)
                        mixed(0)
                        split_tile(2)
                        split_tile(3)
                        mix_lo(0, b_lo, b_hi)
                        split_tile(4)
                        dve.wait_ge(mlo_done, n * 2 + 1 + FIRST)
                        mixed(1)
                        split_tile(5)
                        dve.wait_ge(mix_done, (n * 2 + 2) * ET)
                        if blk < NB - 1:
                            nc.vector.tensor_copy(xf[:, :, 0:1], xf[:, :, BLK:BLK + 1]).then_inc(col_zero, 1)
                        else:
                            nc.vector.memset(xf[:, :, 0:1], 0.0).then_inc(col_zero, 1)
                        s = (blk + 1) % 2
                        moments(xb[s], s, i * 32 + (16 if s else 32) + 16 * ((blk - (1 - s)) // 2 if s else (blk - 1) // 2), n + 1)
                        split_tile(6)
                        split_tile(7)
                        normalise(xb[s], n + 1)
                        mix_lo(1, a_lo, a_hi)

                        def to_gate(t):
                            dve.wait_ge(tanh_done, n * TT + t + 1 + FIRST)
                            nc.vector.tensor_scalar(gate[:, t, :], gate[:, t, :], 0.5, 0.5, ALU.mult, ALU.add)\
                                .then_inc(gate_done, 1)

                        def key(t):
                            dve.wait_ge(relu_done, n * TT + t + 1 + FIRST)
                            nc.vector.tensor_tensor(relu[t % 2][:], relu[t % 2][:], relu[t % 2][:], ALU.mult)\
                                .then_inc(sq_done, 1)

                        def key_lo(t):
                            dve.wait_ge(chi_done, n * TT + t + 1)
                            nc.vector.tensor_tensor(b_lo[:, t, :], relu[t % 2][:], b_hi[:, t, :].bitcast(F32),
                                                    ALU.subtract).then_inc(clo_done, 1)

                        to_gate(0)
                        to_gate(1)
                        to_gate(2)
                        to_gate(3)
                        key(0)
                        key(1)
                        key_lo(0)
                        key(2)
                        key_lo(1)
                        key(3)
                        key_lo(2)
                        key_lo(3)
                        split_xn(n + 1)
                        dve.wait_ge(gate_done, (n + 1) * TT)
                        for t in range(TT):
                            c = blk * TT + t
                            dve.wait_ge(tile_done, tile0 + F0 + t + 1)
                            dve.wait_ge(part_stored[c % 2], i * (NB * TT // 2 * 16) + 16 * (c // 2) + DMA_FIRST)
                            nc.vector.tensor_tensor(f_out[c % 2][:], ring[(blk * NT + F0 + t) % RING][:],
                                                    gate[:, t, :], ALU.mult).then_inc(f_done, 1)

            @block.tensor
            def _(pe):
                def transposes(n, first=False):
                    pe.wait_ge(xn_done, (n + 1) * TT)
                    for e in range(ET):
                        if e >= 2:
                            pe.wait_ge(xf_done, n * ET + e - 1)
                        elif e == 0 and not first:
                            pe.wait_ge(xf_done, n * ET)
                        for t in range(TT):
                            last = nc.tensor.transpose(tps[e % 2][:, t * P:(t + 1) * P], xn[:, t, e * P:(e + 1) * P],
                                                       ident[:])
                        last.then_inc(t_done, 1)

                def product(n0, m, pairs, operand=None):
                    wait_ring(pe, n0, m)
                    out = ring[(n0[1] * NT + m) % RING]
                    for k, (lhs, rhs) in enumerate(pairs):
                        if operand and k % 3 == 0:
                            pe.wait_ge(operand[0], operand[1] + k // 3 + 1)
                        last = nc.tensor.matmul(out[:], lhs, rhs, start=(k == 0), stop=(k == len(pairs) - 1))
                    last.then_inc(tile_done, 1)

                def channels_out(a, w, cols):
                    return [(wx[:, e, cols], ax[:, e, :]) for e in range(ET)
                            for wx, ax in ((w_hi[w], a[0]), (w_hi[w], a[1]), (w_lo[w], a[0]))]

                def tokens_out(a, w, cols):
                    return [(ax[:, e, cols], wx[:, e, :]) for e in range(ET)
                            for ax, wx in ((a[0], w_hi[w]), (a[0], w_lo[w]), (a[1], w_hi[w]))]

                a, b = (a_hi, a_lo), (b_hi, b_lo)
                tile = [slice(t * P, (t + 1) * P) for t in range(4)]
                pe.wait_ge(ident_set, 1)
                transposes(0, first=True)
                pe.wait_ge(w_split, 6)
                with pe.Fori(0, B) as i:
                    for blk in range(NB):
                        n = i * NB + blk
                        n0 = (i, blk)
                        for g in range(G):
                            product(n0, Q0 + g, channels_out(a, 0, tile[g]), (xlo_done, n * ET) if g == 0 else None)
                        for g in range(G):
                            product(n0, K0 + g, channels_out(a, 1, tile[g]))
                        for t in range(TT):
                            product(n0, V0 + t, tokens_out(a, 2, tile[t]))
                        pe.wait_ge(mlo_done, n * 2 + 1 + FIRST)
                        for t in range(TT):
                            product(n0, R0 + t, tokens_out(b, 3, tile[t]))
                        pe.wait_ge(mlo_done, n * 2 + 2 + FIRST)
                        for t in range(TT):
                            product(n0, C0 + t, channels_out(a, 4, tile[t]))
                        transposes(n + 1)
                        for t in range(TT):
                            product(n0, F0 + t, tokens_out(b, 5, tile[t]),
                                    (clo_done, n * TT + FIRST) if t == 0 else None)


def attention(nc, q_hi, q_lo, k_hi, k_lo, v_all, ctx_t):
    NG = B * G
    KT = T // P
    STEPS = [TT * (j + 1) for j in range(NB)]
    S0 = [sum(STEPS[:j]) for j in range(NB)]
    NSTEP = sum(STEPS)
    NPAIR = NSTEP // 2
    NPR = 4
    CH = [HG * TT * (j + 1) + 1 for j in range(NB)]
    C0 = [sum(CH[:j]) for j in range(NB)]
    NCH = sum(CH)
    NTAKE = NCH - NB
    with ExitStack() as ctx:
        def sb(name, shape, dt=F32):
            return ctx.enter_context(nc.sbuf_tensor(name, shape, dt))

        def sem(name):
            return ctx.enter_context(nc.semaphore(name))

        qs = [sb(f"q_stack{s}", [P, HG, T], F32R) for s in range(2)]
        ks = [sb(f"k_stack{s}", [P, HG, T], F32R) for s in range(2)]
        vs = [sb(f"v_group{s}", [P, KT, P]) for s in range(2)]
        pr = [sb(f"probs{s}", [P, HG, BLK]) for s in range(NPR)]
        o_sb = [sb(f"o_sb{s}", [P, BLK]) for s in range(2)]
        s_sb = [sb(f"s_sb{s}", [P, BLK]) for s in range(2)]
        o_n = [sb(f"o_norm{s}", [P, BLK]) for s in range(2)]
        tri = sb("tri", [P, BLK])
        junk = [sb(f"junk{s}", [P, BLK]) for s in range(2)]
        m_part = sb("m_part", [P, HG * TT, NB])
        m_neg = [sb(f"m_neg{s}", [P, HG * TT]) for s in range(2)]
        m_row = [sb(f"m_row{s}", [HG * TT, P], F32R) for s in range(2)]
        ident = sb("ident2", [P, P])
        ident_b = sb("ident_b", [P, P], BF16)
        tri_b = sb("tri_b", [P, P], BF16)
        ones = sb("ones", [P, HD])
        sT = [ctx.enter_context(nc.psum_tensor(f"scores_t{h}", [P, BLK], F32)) for h in range(HG)]
        mx = [ctx.enter_context(nc.psum_tensor(f"scores{s}", [P, BLK], F32)) for s in range(2)]
        o_ps = ctx.enter_context(nc.psum_tensor("o_ps", [P, BLK], F32))
        s_ps = ctx.enter_context(nc.psum_tensor("s_ps", [P, BLK], F32))

        q_ld = [[sem(f"q_loaded{s}{j}") for j in range(NB)] for s in range(2)]
        kv_ld = [[sem(f"kv_loaded{s}{j}") for j in range(NB)] for s in range(2)]
        m_ld = [sem(f"m_loaded{j}") for j in range(NB)]
        o_st = [sem(f"o_stored{s}") for s in range(2)]
        cst0 = sem("const_base")
        cst = sem("const_ready")
        one_rows = sem("one_rows_ready")
        mm_done = sem("chunk_done")
        mx_freed = sem("chunk_taken")
        neg_done = sem("m_neg_ready")
        row_done = sem("m_row_ready")
        qk_done = sem("scores_t_done")
        ex_done = sem("probs_done")
        pv_done = sem("pv_done")
        pair_done = sem("pair_added")
        sm_done = sem("sum_done")
        o_cp = sem("o_copied")
        s_cp = sem("s_copied")
        rc_done = sem("recip_done")
        on_done = sem("o_norm_done")

        LINE = [(par, j, kt, S0[j] + kt) for par in range(2) for j in range(NB) for kt in range(STEPS[j])]
        ENDS = [x for x, (par, j, kt, n) in enumerate(LINE) if kt == STEPS[j] - 1]

        with nc.Block() as block:
            def load_q(sp, g, par, j):
                src = [a[bass.ds(g * P, P), j * BLK:(j + 1) * BLK].rearrange("(h d) t -> d h t", h=HG)
                       for a in (q_hi, q_hi, q_lo)]
                for c in range(3):
                    sp.dma_start(qs[par][c * HD:(c + 1) * HD, :, j * BLK:(j + 1) * BLK].bitcast(F32), src[c]
                                 ).then_inc(q_ld[par][j], 16)

            def load_kv(sp, g, par, j):
                src = [a[bass.ds(g * P, P), j * BLK:(j + 1) * BLK].rearrange("(h d) t -> d h t", h=HG)
                       for a in (k_hi, k_lo, k_hi)]
                for c in range(3):
                    sp.dma_start(ks[par][c * HD:(c + 1) * HD, :, j * BLK:(j + 1) * BLK].bitcast(F32), src[c]
                                 ).then_inc(kv_ld[par][j], 16)
                sp.dma_start(vs[par][:, j * TT:(j + 1) * TT, :],
                             v_all[bass.ds(g * T + j * BLK, BLK), :].rearrange("(t p) c -> p t c", p=P)
                             ).then_inc(kv_ld[par][j], 16)

            def store_m(sp, mg, j):
                par, u = mg_par[0], j % 2
                sp.wait_ge(row_done, mg * NB + j + 1 + FIRST)
                for h in range(HG):
                    sp.dma_start(qs[par][QK_ROWS:QK_ROWS + 1, h, j * BLK:(j + 1) * BLK].bitcast(F32),
                                 m_row[u][h * TT:(h + 1) * TT, :].bitcast(F32)).then_inc(m_ld[j], 16)

            mg_par = [0]

            @block.sync
            def _(sp):
                start_counters(sp, [on_done, sm_done, row_done, ex_done, o_cp, s_cp], o_st)
                for j in range(NB):
                    load_kv(sp, 0, 0, j)
                    load_q(sp, 0, 0, j)
                for j in range(NB):
                    load_kv(sp, 1, 1, j)
                    load_q(sp, 1, 1, j)
                mg_par[0] = 0
                for j in range(NB):
                    store_m(sp, 0, j)

                def store_o(g0, u):
                    par, j = divmod(u, NB)
                    sp.wait_ge(on_done, g0 * NB + u + 1 + FIRST)
                    sp.dma_start(ctx_t[bass.ds((g0 + par) * P, P), j * BLK:(j + 1) * BLK], o_n[u % 2][:]
                                 ).then_inc(o_st[u % 2], 16)

                def body(g0, last):
                    for par in range(2):
                        g = g0 + par
                        for j in range(NB):
                            u = par * NB + j
                            if not last:
                                if j == NB - 1:
                                    for c in range(NB - 1):
                                        sp.wait_ge(pv_done, g * NSTEP + S0[j] + (c + 1) * TT)
                                        load_kv(sp, g + 2, par, c)
                            if u >= 1:
                                store_o(g0, u - 1)
                            if not (last and par == 1):
                                mg_par[0] = 1 - par
                                store_m(sp, g + 1, j)
                            if not last:
                                sp.wait_ge(qk_done, g * (NSTEP * HG) + (S0[j] + STEPS[j]) * HG)
                                load_q(sp, g + 2, par, j)
                        if not last:
                            sp.wait_ge(pv_done, (g + 1) * NSTEP)
                            load_kv(sp, g + 2, par, NB - 1)
                    store_o(g0, 2 * NB - 1)

                with sp.Fori(0, NG // 2 - 1) as i:
                    body(2 * i, False)
                body(NG - 2, True)
                for s in range(2):
                    sp.wait_ge(o_st[s], NG * NB // 2 * 16 + DMA_FIRST)

            @block.gpsimd
            def _(pool):
                nc.gpsimd.memset(ones[:], 1.0).then_inc(cst, 1)
                nc.gpsimd.memset(ident[:], 1.0).then_inc(cst0, 1)
                nc.gpsimd.memset(tri[:], 0.0).then_inc(cst0, 1)
                nc.gpsimd.memset(ident_b[:], 1.0).then_inc(cst0, 1)
                nc.gpsimd.memset(tri_b[:], 0.0).then_inc(cst0, 1)
                pool.wait_ge(cst0, 4)
                nc.gpsimd.affine_select(out=ident_b[:], in_=ident_b[:], compare_op=ALU.is_equal, fill=0.0, base=0,
                                        pattern=[[-1, P]], channel_multiplier=1).then_inc(cst, 1)
                nc.gpsimd.affine_select(out=tri_b[:], in_=tri_b[:], compare_op=ALU.is_ge, fill=MASKED, base=0,
                                        pattern=[[1, P]], channel_multiplier=-1).then_inc(cst, 1)
                nc.gpsimd.affine_select(out=ident[:], in_=ident[:], compare_op=ALU.is_equal, fill=0.0, base=0,
                                        pattern=[[-1, P]], channel_multiplier=1).then_inc(cst, 1)
                nc.gpsimd.affine_select(out=tri[:, BLK - P:BLK], in_=tri[:, BLK - P:BLK], compare_op=ALU.is_ge,
                                        fill=MASKED, base=0, pattern=[[-1, P]], channel_multiplier=1).then_inc(cst, 1)
                pool.wait_ge(cst, 5)
                for s in range(2):
                    pool.wait_ge(one_rows, s)
                    nc.gpsimd.memset(ks[s][QK_ROWS:QK_ROWS + 1, :, :].bitcast(F32), 1.0).then_inc(one_rows, 1)
                pool.wait_ge(one_rows, 2)

                def body(g0):
                    def scale_o(u):
                        pool.wait_ge(rc_done, (g0 * NB + u + 1) * TT)
                        pool.wait_ge(o_st[u % 2], (g0 * NB + u - u % 2) * 8 + DMA_FIRST)
                        nc.gpsimd.tensor_tensor(o_n[u % 2][:], o_sb[u % 2][:], s_sb[u % 2][:], ALU.mult)\
                            .then_inc(on_done, 1)

                    for x, (par, j, kt, n) in enumerate(LINE):
                        g = g0 + par
                        if n % 2 == 1 and x < len(LINE) - 1:
                            col = max(kt - j * TT, 0) * P
                            pool.wait_ge(ex_done, g * (NSTEP * HG) + (n + 1) * HG + FIRST)
                            pool.wait_ge(pv_done, g * NSTEP + n)
                            even, odd = pr[(n - 1) % NPR], pr[n % NPR]
                            nc.gpsimd.tensor_tensor(even[:, :, col:], even[:, :, col:], odd[:, :, col:], ALU.add)\
                                .then_inc(pair_done, 1)
                        if x - 6 in ENDS:
                            scale_o(ENDS.index(x - 6))
                    scale_o(2 * NB - 1)

                with pool.Fori(0, NG // 2 - 1) as i:
                    body(2 * i)
                body(NG - 2)

            @block.scalar
            def _(act):
                def body(g0):
                    def copy_o(u):
                        par, j = divmod(u, NB)
                        act.wait_ge(on_done, g0 * NB + max(u - 1, 0) + FIRST)
                        act.wait_ge(pv_done, (g0 + par) * NSTEP + S0[j] + STEPS[j])
                        nc.scalar.activation(o_sb[u % 2][:], o_ps[:], ACT.Copy).then_inc(o_cp, 1)

                    def copy_s(u):
                        par, j = divmod(u, NB)
                        act.wait_ge(sm_done, (g0 + par) * NPAIR + (S0[j] + STEPS[j]) // 2 + FIRST)
                        nc.scalar.activation(s_sb[u % 2][:], s_ps[:], ACT.Copy).then_inc(s_cp, 1)

                    for x, (par, j, kt, n) in enumerate(LINE):
                        g = g0 + par
                        col = max(kt - j * TT, 0) * P
                        pairs = (n - NPR) // 2 + 1
                        act.wait_ge(sm_done, g * NPAIR + (pairs if pairs > 0 or par == 1 else 0) + FIRST)
                        for h in range(HG):
                            act.wait_ge(qk_done, g * (NSTEP * HG) + n * HG + h + 1)
                            nc.scalar.activation(pr[n % NPR][:, h, col:], sT[h][:, col:], ACT.Exp,
                                                 scale=SCALE).then_inc(ex_done, 1)
                        if x - 1 in ENDS:
                            copy_o(ENDS.index(x - 1))
                        if x - 2 in ENDS:
                            copy_s(ENDS.index(x - 2))
                    copy_o(2 * NB - 1)
                    copy_s(2 * NB - 1)

                with act.Fori(0, NG // 2 - 1) as i:
                    body(2 * i)
                body(NG - 2)

            def chunks(j):
                return [(h, r, c) for h in range(HG) for r in range(TT) for c in range(j + 1)]

            @block.vector
            def _(dve):
                dve.wait_ge(cst, 5)

                def take_chunk(mg, j, idx):
                    h, r, c = chunks(j)[idx]
                    e = C0[j] + idx
                    dve.wait_ge(mm_done, mg * NCH + e + 1)
                    dst = m_part[:, h * TT + r, c:c + 1]
                    if c < j:
                        nc.vector.tensor_reduce(dst, mx[e % 2][:], AX_X, ALU.max).then_inc(mx_freed, 1)
                    else:
                        w = (r + 1) * P
                        dve.nop(nofuse=True)
                        nc.vector.tensor_tensor_reduce(
                            out=junk[idx % 2][:, 0:w], in0=mx[e % 2][:, 0:w], in1=tri[:, BLK - w:BLK], scale=1.0,
                            scalar=MASKED, op0=ALU.add, op1=ALU.max, accum_out=dst).then_inc(mx_freed, 1)

                def negate(mg, j):
                    dve.wait_ge(mx_freed, mg * NTAKE + C0[j] - j + CH[j] - 1)
                    nc.vector.tensor_reduce(m_neg[j % 2][:], m_part[:, :, 0:j + 1], AX_X, ALU.max, negate=True)\
                        .then_inc(neg_done, 1)

                def take_rows(mg, j, first=False):
                    e = C0[j] + CH[j] - 1
                    dve.wait_ge(mm_done, mg * NCH + e + 1)
                    if j >= 2:
                        dve.wait_ge(m_ld[j - 2], (mg + 1) * (HG * 16))
                    elif not first:
                        dve.wait_ge(m_ld[j + 2], mg * (HG * 16))
                    nc.vector.tensor_copy(m_row[j % 2][:], mx[e % 2][0:HG * TT, 0:P]).then_inc(row_done, 1)

                for j in range(NB):
                    for idx in range(CH[j] - 1):
                        take_chunk(0, j, idx)
                    negate(0, j)
                    take_rows(0, j, first=True)

                def body(g0, last):
                    def invert(u, piece):
                        dve.wait_ge(s_cp, g0 * NB + u + 1 + FIRST)
                        s = s_sb[u % 2][:, piece * P:(piece + 1) * P]
                        nc.vector.reciprocal(s, s).then_inc(rc_done, 1)

                    for x, (par, j, kt, n) in enumerate(LINE):
                        mg = g0 + par + 1
                        if not (last and par == 1):
                            for k in range(HG):
                                take_chunk(mg, j, kt * HG + k)
                            if kt == STEPS[j] - 1:
                                negate(mg, j)
                                take_rows(mg, j)
                        for piece in range(TT):
                            if x - 2 - piece in ENDS:
                                invert(ENDS.index(x - 2 - piece), piece)
                    for piece in range(TT):
                        invert(2 * NB - 1, piece)

                with dve.Fori(0, NG // 2 - 1) as i:
                    body(2 * i, False)
                body(NG - 2, True)

            @block.tensor
            def _(pe):
                pe.wait_ge(cst, 5)

                def max_chunk(mg, mpar, loads, j, idx, first=False):
                    h, r, c = chunks(j)[idx]
                    e = C0[j] + idx
                    if idx == 1:
                        pe.wait_ge(row_done, mg * NB + j + FIRST)
                    if idx == 0:
                        pe.wait_ge(kv_ld[mpar][j], loads * 64)
                        pe.wait_ge(q_ld[mpar][j], loads * 48)
                    taken = e - j - (1 if idx >= 1 else 0)
                    if taken > 0 or not first:
                        pe.wait_ge(mx_freed, mg * NTAKE + max(taken, 0))
                    w = BLK if c < j else max((r + 1) * P, 2 * P)
                    q0 = j * BLK + r * P
                    nc.tensor.matmul(mx[e % 2][:, 0:w], qs[mpar][0:QK_ROWS, h, q0:q0 + P],
                                     ks[mpar][0:QK_ROWS, h, c * BLK:c * BLK + w], start=True, stop=True)\
                        .then_inc(mm_done, 1)

                def max_rows(mg, j):
                    e = C0[j] + CH[j] - 1
                    pe.wait_ge(neg_done, mg * NB + j + 1)
                    nc.tensor.transpose(mx[e % 2][0:HG * TT, 0:P], m_neg[j % 2][:], ident[:]).then_inc(mm_done, 1)

                for j in range(NB):
                    for idx in range(CH[j] - 1):
                        max_chunk(0, 0, 1, j, idx, first=True)
                    max_rows(0, j)

                pe.wait_ge(one_rows, 2)

                def body(i, g0, last):
                    def scores(par, j, kt, h):
                        g, n = g0 + par, S0[j] + kt
                        if kt == 0 and h == 0:
                            pe.wait_ge(m_ld[j], (g + 1) * (HG * 16))
                        done = n * HG + h + 1 - HG
                        pe.wait_ge(ex_done, g * (NSTEP * HG) + (done if done > 0 or par == 1 else 0) + FIRST)
                        col = min(max(kt - j * TT, 0) * P, BLK - 2 * P)
                        last = nc.tensor.matmul(sT[h][:, col:], ks[par][0:QK_ROWS + 1, h, kt * P:(kt + 1) * P],
                                         qs[par][0:QK_ROWS + 1, h, j * BLK + col:(j + 1) * BLK],
                                         start=True, stop=True)
                        if kt >= j * TT:
                            d = (kt - j * TT) * P
                            last = nc.tensor.matmul(sT[h][:, d:d + P], ident_b[:], tri_b[:], start=False, stop=True,
                                                    skip_group_check=True)
                        last.then_inc(qk_done, 1)

                    def side_by_side(dst, par, j, kt, lhs, stop):
                        col = max(kt - j * TT, 0) * P
                        for h in range(HG):
                            last = nc.tensor.matmul(dst[h * HD:(h + 1) * HD, col:], lhs[h],
                                                    pr[(S0[j] + kt) % NPR][:, h, col:], start=(kt == 0), stop=stop)
                        return last

                    def weigh(par, j, kt, n):
                        g = g0 + par
                        pe.wait_ge(ex_done, g * (NSTEP * HG) + (n + 1) * HG + FIRST)
                        if kt == 0:
                            pe.wait_ge(o_cp, g * NB + j + FIRST)
                        side_by_side(o_ps, par, j, kt, [vs[par][:, kt, h * HD:(h + 1) * HD] for h in range(HG)],
                                     kt == STEPS[j] - 1).then_inc(pv_done, 1)

                    def total(par, j, kt, n, alone=False):
                        g = g0 + par
                        if kt == 0:
                            pe.wait_ge(s_cp, g * NB + j + FIRST)
                        if not alone:
                            pe.wait_ge(pair_done, i * (2 * NPAIR - 1) + par * NPAIR + n // 2 + 1)
                        last = side_by_side(s_ps, par, j, kt, [ones[:]] * HG, kt == STEPS[j] - 2 and not alone)
                        if alone:
                            last = side_by_side(s_ps, par, j, kt + 1, [ones[:]] * HG, True)
                        last.then_inc(sm_done, 1)

                    for x, (par, j, kt, n) in enumerate(LINE):
                        for h in range(HG):
                            scores(par, j, kt, h)
                            if not (last and par == 1):
                                max_chunk(g0 + par + 1, 1 - par, i + 1 + par, j, kt * HG + h)
                            if x >= 1 and h == 1:
                                weigh(*LINE[x - 1])
                        if x >= 3 and x % 2 == 1:
                            total(*LINE[x - 3])
                        if kt == STEPS[j] - 1 and not (last and par == 1):
                            max_rows(g0 + par + 1, j)
                    weigh(*LINE[-1])
                    total(*LINE[-2], alone=True)

                with pe.Fori(0, NG // 2 - 1) as i:
                    body(i, 2 * i, False)
                body(NG // 2 - 1, NG - 2, True)


def project_out(nc, ctx_t, w_o, part, out):
    NBLK = B * NB
    with ExitStack() as ctx:
        def sb(name, shape, dt=F32):
            return ctx.enter_context(nc.sbuf_tensor(name, shape, dt))

        def sem(name):
            return ctx.enter_context(nc.semaphore(name))

        w_raw = sb("wo_raw", [P, ET, D])
        w_hi = sb("wo_hi", [P, ET, D], F32R)
        w_lo = sb("wo_lo", [P, ET, D], F32R)
        c_raw = [sb(f"ctx{s}", [P, ET, BLK]) for s in range(2)]
        c_hi = [sb(f"ctx_hi{s}", [P, ET, BLK], F32R) for s in range(2)]
        c_lo = [sb(f"ctx_lo{s}", [P, ET, BLK], F32R) for s in range(2)]
        res = [sb(f"res{s}", [P, TT, D]) for s in range(2)]
        ps = [ctx.enter_context(nc.psum_tensor(f"out_ps{s}", [P, D], F32)) for s in range(2 * TT)]
        w_ld = sem("wo_loaded")
        whi = sem("wo_hi_ready")
        wlo = sem("wo_lo_ready")
        c_ld = [sem(f"ctx_loaded{s}") for s in range(2)]
        r_ld = [sem(f"res_loaded{s}") for s in range(2)]
        chi = sem("ctx_hi_ready")
        clo = sem("ctx_lo_ready")
        done = sem("out_tile_done")
        added = sem("out_added")
        stored = [sem(f"out_stored{s}") for s in range(2)]

        with nc.Block() as block:
            @block.sync
            def _(sp):
                start_counters(sp, [clo, done, added], stored)
                sp.dma_start(w_raw[:], w_o.rearrange("(t p) a -> p t a", p=P)).then_inc(w_ld, 16)
                with sp.Fori(0, B) as i:
                    for j in range(NB):
                        s = j % 2
                        n = i * NB + j
                        half = i * (NB // 2) + j // 2
                        if j >= 2:
                            sp.wait_ge(clo, n - 1 + FIRST)
                        else:
                            sp.wait_ge(clo, i * NB + FIRST)
                        sp.dma_start(c_raw[s][:], ctx_t[bass.ds(i * (G * P), G * P), j * BLK:(j + 1) * BLK]
                                     .rearrange("(g p) t -> p g t", p=P)).then_inc(c_ld[s], 16)
                        sp.wait_ge(stored[s], half * 16 + DMA_FIRST)
                        sp.dma_start(res[s][:], part[bass.ds(i * T + j * BLK, BLK), :]
                                     .rearrange("(t p) d -> p t d", p=P)).then_inc(r_ld[s], 16)
                for s in range(2):
                    sp.wait_ge(stored[s], NBLK // 2 * 16 + DMA_FIRST)

            @block.scalar
            def _(act):
                act.wait_ge(w_ld, 16)
                nc.scalar.activation(w_hi[:], w_raw[:], ACT.Copy).then_inc(whi, 1)
                with act.Fori(0, B) as i:
                    for j in range(NB):
                        s = j % 2
                        n = i * NB + j
                        half = i * (NB // 2) + j // 2
                        act.wait_ge(c_ld[s], half * 16 + 16)
                        act.wait_ge(done, (i * NB + max(j - 1, 0)) * TT + FIRST)
                        nc.scalar.activation(c_hi[s][:], c_raw[s][:], ACT.Copy).then_inc(chi, 1)
                        if j >= 1:
                            act.wait_ge(added, n * TT + FIRST)
                            act.dma_start(out[bass.ds(i * T + (j - 1) * BLK, BLK), :]
                                          .rearrange("(t p) d -> p t d", p=P), res[1 - s][:]).then_inc(stored[1 - s], 16)
                    act.wait_ge(added, (i + 1) * (NB * TT) + FIRST)
                    act.dma_start(out[bass.ds(i * T + (NB - 1) * BLK, BLK), :]
                                  .rearrange("(t p) d -> p t d", p=P), res[1][:]).then_inc(stored[1], 16)

            @block.gpsimd
            def _(pool):
                with pool.Fori(0, B) as i:
                    for j in range(NB):
                        s = j % 2
                        pool.wait_ge(chi, i * NB + j + 1)
                        nc.gpsimd.tensor_tensor(c_lo[s][:], c_raw[s][:], c_hi[s][:].bitcast(F32), ALU.subtract)\
                            .then_inc(clo, 1)

            @block.vector
            def _(dve):
                dve.wait_ge(whi, 1)
                nc.vector.tensor_tensor(w_lo[:], w_raw[:], w_hi[:].bitcast(F32), ALU.subtract).then_inc(wlo, 1)

                with dve.Fori(0, B) as i:
                    for j in range(NB):
                        s = j % 2
                        n = i * NB + j
                        half = i * (NB // 2) + j // 2
                        dve.wait_ge(r_ld[s], half * 16 + 16)
                        for t in range(TT):
                            dve.wait_ge(done, n * TT + t + 1 + FIRST)
                            nc.vector.tensor_tensor(res[s][:, t, :], ps[s * TT + t][:], res[s][:, t, :], ALU.add)\
                                .then_inc(added, 1)

            @block.tensor
            def _(pe):
                pe.wait_ge(wlo, 1)
                with pe.Fori(0, B) as i:
                    for j in range(NB):
                        s = j % 2
                        n = i * NB + j
                        pe.wait_ge(clo, n + 1 + FIRST)
                        pe.wait_ge(added, (i * NB + max(j - 1, 0)) * TT + FIRST)
                        for t in range(TT):
                            pairs = [(ax[:, e, t * P:(t + 1) * P], wx[:, e, :]) for e in range(ET)
                                     for ax, wx in ((c_hi[s], w_hi), (c_hi[s], w_lo), (c_lo[s], w_hi))]
                            for k, (lhs, rhs) in enumerate(pairs):
                                last = nc.tensor.matmul(ps[s * TT + t][:], lhs, rhs, start=(k == 0),
                                                        stop=(k == len(pairs) - 1))
                            last.then_inc(done, 1)


def build_program(nc, x, w_t, w_o, b_o, mu_r, mu_k, out):
    def scratch(name, shape, dt=F32):
        return nc.dram_tensor(name, shape, dt, kind="Internal").ap()

    split = [scratch(n, [B * G * P, T]) for n in ("q_hi", "q_lo", "k_hi", "k_lo")]
    v_all = scratch("v_all", [B * G * T, P])
    part = scratch("part", [B * T, D])
    ctx_t = scratch("ctx_t", [B * G * P, T])
    project_and_ffn(nc, x, w_t, b_o, mu_r, mu_k, *split, v_all, part)
    attention(nc, *split, v_all, ctx_t)
    project_out(nc, ctx_t, w_o, part, out)


def kernel(**inputs):
    import numpy as _np
    import concourse.bacc as _bacc
    from concourse import mybir as _mybir
    from concourse.bass_utils import run_bass_kernel_spmd as _run

    nc = _bacc.Bacc("TRN2", target_bir_lowering=False, num_devices=1)
    nc.disable_value_cache = True
    a = {k: _np.asarray(v) for k, v in inputs.items()}
    laid = {
        "x": a["L0_attn_x"].reshape(B * T, D),
        "b_o": _np.broadcast_to(a["L0_attn_b_o"], (P, D)),
        "mu_r": a["L0_ffn_mu_r"].reshape(ET, P).T,
        "mu_k": a["L0_ffn_mu_k"].reshape(ET, P).T,
    }
    names = ["L0_attn_W_q", "L0_attn_W_k", "L0_attn_W_v", "L0_ffn_W_r", "L0_ffn_W_k", "L0_ffn_W_v", "L0_attn_W_o"]
    for n, name in enumerate(names):
        laid[f"w{n}"] = a[name].T
    laid = {k: _np.ascontiguousarray(v) for k, v in laid.items()}
    h = {k: nc.dram_tensor(f"in_{k}", v.shape, _mybir.dt.from_np(v.dtype), kind="ExternalInput").ap()
         for k, v in laid.items()}
    out = nc.dram_tensor("out_0", (B * T, D), _mybir.dt.float32, kind="ExternalOutput").ap()
    build_program(nc, h["x"], [h[f"w{n}"] for n in range(6)], h["w6"], h["b_o"], h["mu_r"], h["mu_k"], out)
    r = _run(nc, [{f"in_{k}": v for k, v in laid.items()}], core_ids=[0])
    return r.results[0]["out_0"].reshape(B, T, D)
```

```python
from contextlib import ExitStack

import concourse.bass as bass
from concourse import mybir

F32 = mybir.dt.float32
F32R = mybir.dt.float32r
BF16 = mybir.dt.bfloat16
ALU = mybir.AluOpType
ACT = mybir.ActivationFunctionType
AX_X = mybir.AxisListType.X

P = 128
B, T, D = 4, 2048, 512
H, HD = 16, 32
HG = P // HD
G = H // HG
BLK = 512
NB = T // BLK
ET = D // P
TT = BLK // P
QK_ROWS = 3 * HD
SCALE = float(HD) ** -0.5
EPS = 1e-5
MASKED = -1e30

FIRST = 1
DMA_FIRST = 16



def start_counters(eng, counters, dma_counters):
    for c in counters:
        eng.sem_inc(c, FIRST)
    for c in dma_counters:
        eng.sem_inc(c, DMA_FIRST)


def project_and_ffn(nc, x, w_t, b_o, mu_r, mu_k, q_hi, q_lo, k_hi, k_lo, v_all, part):
    NT = 2 * G + 4 * TT
    RING = 6
    Q0, K0, V0, R0, C0, F0 = 0, G, 2 * G, 2 * G + TT, 2 * G + 2 * TT, 2 * G + 3 * TT
    NS = 4
    with ExitStack() as ctx:
        def sb(name, shape, dt=F32):
            return ctx.enter_context(nc.sbuf_tensor(name, shape, dt))

        def sem(name):
            return ctx.enter_context(nc.semaphore(name))

        w_hi = [sb(f"w_hi{n}", [P, ET, D], F32R) for n in range(6)]
        w_lo = [sb(f"w_lo{n}", [P, ET, D], F32R) for n in range(6)]
        xb = [sb(f"x_block{s}", [P, TT, D]) for s in range(2)]
        xn = sb("xn", [P, TT, D])
        xf = sb("xn_t", [P, ET, BLK + 1])
        mix = sb("mix", [P, ET, BLK])
        a_hi = sb("a_hi", [P, ET, BLK], F32R)
        a_lo = sb("a_lo", [P, ET, BLK], F32R)
        b_hi = sb("b_hi", [P, ET, BLK], F32R)
        b_lo = sb("b_lo", [P, ET, BLK], F32R)
        st_hi = [sb(f"st_hi{s}", [P, BLK], F32R) for s in range(NS)]
        st_lo = [sb(f"st_lo{s}", [P, BLK], F32R) for s in range(NS)]
        v_st = [sb(f"v_st{s}", [P, D]) for s in range(2)]
        gate = sb("gate", [P, TT, D])
        relu = [sb(f"relu{s}", [P, BLK]) for s in range(2)]
        f_out = [sb(f"f_out{s}", [P, D]) for s in range(2)]
        bias = sb("bias", [P, D])
        mus = sb("mus", [P, 2, ET])
        ident = sb("ident", [P, P])
        stats = sb("stats", [P, TT, 6])
        mean_var = sb("mean_var", [P, TT, 2])
        var_eps = sb("var_eps", [P, TT])
        sd = sb("sd", [P, TT])
        rstd = sb("rstd", [P, TT])
        ring = [ctx.enter_context(nc.psum_tensor(f"ring{s}", [P, BLK], F32)) for s in range(RING)]
        tps = [ctx.enter_context(nc.psum_tensor(f"tps{s}", [P, BLK], F32)) for s in range(2)]

        w_ld = [sem(f"w_loaded{s}") for s in range(2)]
        w_split_hi = sem("w_split_hi")
        w_split = sem("w_split")
        small_ld = sem("small_loaded")
        x_ld = [sem(f"x_loaded{s}") for s in range(2)]
        ones_set = sem("ones_set")
        ident_set = sem("ident_set")
        stats_done = sem("stats_done")
        aggr_done = sem("aggr_done")
        var_done = sem("var_done")
        sd_done = sem("sd_done")
        rstd_done = sem("rstd_done")
        xn_done = sem("xn_done")
        res_done = sem("residual_done")
        t_done = sem("transposed")
        xf_done = sem("xn_t_ready")
        xhi_done = sem("xn_hi_ready")
        xlo_done = sem("xn_lo_ready")
        col_zero = sem("column0_ready")
        step_done = sem("step_ready")
        mix_done = sem("mix_ready")
        mhi_done = sem("mix_hi_ready")
        mlo_done = sem("mix_lo_ready")
        tile_done = sem("tile_done")
        qk_done = sem("qk_split")
        st_hi_done = sem("stage_hi")
        stored = [sem(f"stage_stored{s}") for s in range(NS)]
        v_done = sem("v_done")
        v_stored = [sem(f"v_stored{s}") for s in range(2)]
        tanh_done = sem("tanh_done")
        gate_done = sem("gate_done")
        relu_done = sem("relu_done")
        sq_done = sem("square_done")
        chi_done = sem("key_hi_ready")
        clo_done = sem("key_lo_ready")
        f_done = sem("f_done")
        part_done = sem("part_done")
        part_stored = [sem(f"part_stored{s}") for s in range(2)]

        LAST_READER = [(qk_done, Q0, 2 * G), (v_done, V0, TT), (tanh_done, R0, TT), (relu_done, C0, TT),
                       (f_done, F0, TT)]

        def wait_ring(eng, n0, m):
            i, blk = n0
            prev = blk * NT + m - RING
            for done, first, count in LAST_READER:
                if prev < 0:
                    eng.wait_ge(done, i * (NB * count) + FIRST)
                elif first <= prev % NT < first + count:
                    eng.wait_ge(done, i * (NB * count) + prev // NT * count + prev % NT - first + 1 + FIRST)

        with nc.Block() as block:
            @block.sync
            def _(sp):
                start_counters(sp, [qk_done, v_done, tanh_done, relu_done, f_done, clo_done, mlo_done],
                               stored + v_stored + part_stored)
                sp.dma_start(xb[0][:], x[0:BLK, :].rearrange("(t p) d -> p t d", p=P)).then_inc(x_ld[0], 16)
                sp.dma_start(bias[:], b_o).then_inc(small_ld, 16)
                sp.dma_start(mus[:, 0, :], mu_r).then_inc(small_ld, 16)
                sp.dma_start(mus[:, 1, :], mu_k).then_inc(small_ld, 16)
                for n in range(6):
                    if n >= 2:
                        sp.wait_ge(w_split, n - 1)
                    sp.dma_start((mix, gate)[n % 2][:], w_t[n].rearrange("(t p) a -> p t a", p=P)
                                 ).then_inc(w_ld[n % 2], 16)
                sp.dma_start(xb[1][:], x[BLK:2 * BLK, :].rearrange("(t p) d -> p t d", p=P)).then_inc(x_ld[1], 16)
                with sp.Fori(0, B) as i:
                    for blk in range(NB):
                        for m in range(2 * G):
                            c = blk * 2 * G + m
                            g = m % G
                            hi, lo = (q_hi, q_lo) if m < K0 else (k_hi, k_lo)
                            rows = bass.ds(i * (G * P) + g * P, P)
                            sp.wait_ge(qk_done, i * (NB * 2 * G) + c + 1 + FIRST)
                            for dst, src in ((hi, st_hi), (lo, st_lo)):
                                sp.dma_start(dst[rows, blk * BLK:(blk + 1) * BLK], src[c % NS][:].bitcast(F32)
                                             ).then_inc(stored[c % NS], 16)
                        for t in range(TT):
                            c = blk * TT + t
                            sp.wait_ge(v_done, i * (NB * TT) + c + 1 + FIRST)
                            dst = v_all[bass.ds(i * (G * T), G * T), :].rearrange("(g t) c -> t g c", g=G)
                            sp.dma_start(dst[c * P:(c + 1) * P, :, :],
                                         v_st[c % 2][:].rearrange("p (g c) -> p g c", g=G)
                                         ).then_inc(v_stored[c % 2], 16)
                        for t in range(TT):
                            c = blk * TT + t
                            sp.wait_ge(part_done, i * (NB * TT) + c + 1)
                            sp.dma_start(part[bass.ds(i * T + c * P, P), :], f_out[c % 2][:]
                                         ).then_inc(part_stored[c % 2], 16)
                        nxt = blk + 2
                        row = i * T + nxt * BLK if nxt < NB else ((i + 1) % B) * T + (nxt - NB) * BLK
                        sp.dma_start(xb[blk % 2][:], x[bass.ds(row, BLK), :].rearrange("(t p) d -> p t d", p=P)
                                     ).then_inc(x_ld[blk % 2], 16)
                for s in range(2):
                    sp.wait_ge(x_ld[s], 16 * (B * NB // 2 + 1))
                for s in range(NS):
                    sp.wait_ge(stored[s], B * NB * 2 * G // NS * 32 + DMA_FIRST)
                for s in range(2):
                    sp.wait_ge(v_stored[s], B * NB * TT // 2 * 16 + DMA_FIRST)
                    sp.wait_ge(part_stored[s], B * NB * TT // 2 * 16 + DMA_FIRST)

            @block.gpsimd
            def _(pool):
                nc.gpsimd.memset(ident[:], 1.0).then_inc(ones_set, 1)
                pool.wait_ge(ones_set, 1)
                nc.gpsimd.affine_select(out=ident[:], in_=ident[:], compare_op=ALU.is_equal, fill=0.0, base=0,
                                        pattern=[[-1, P]], channel_multiplier=1).then_inc(ident_set, 1)
                pool.wait_ge(small_ld, 48)

                def residual(buf, n):
                    pool.wait_ge(xn_done, n)
                    for t in range(TT):
                        nc.gpsimd.tensor_tensor(buf[:, t, :], buf[:, t, :], bias[:], ALU.add).then_inc(res_done, 1)

                residual(xb[0], TT)
                with pool.Fori(0, B) as i:
                    for blk in range(NB):
                        n = i * NB + blk
                        residual(xb[(blk + 1) % 2], (n + 2) * TT)
                        for t in range(TT):
                            c = blk * TT + t
                            pool.wait_ge(f_done, i * (NB * TT) + c + 1 + FIRST)
                            pool.wait_ge(res_done, (n + 1) * TT)
                            nc.gpsimd.tensor_tensor(f_out[c % 2][:], f_out[c % 2][:], xb[blk % 2][:, t, :],
                                                    ALU.add).then_inc(part_done, 1)

            @block.scalar
            def _(act):
                def split_w(n):
                    act.wait_ge(w_ld[n % 2], 16 * (n // 2 + 1))
                    nc.scalar.activation(w_hi[n][:], (mix, gate)[n % 2][:], ACT.Copy).then_inc(w_split_hi, 1)

                def root(n):
                    act.wait_ge(var_done, n)
                    nc.scalar.activation(sd[:], var_eps[:], ACT.Sqrt).then_inc(sd_done, 1)

                def take_transposed(n):
                    def hi(e):
                        act.wait_ge(xf_done, n * ET + e + 1)
                        nc.scalar.activation(a_hi[:, e, :], xf[:, e, 1:BLK + 1], ACT.Copy).then_inc(xhi_done, 1)
                    for e in range(ET):
                        act.wait_ge(t_done, n * ET + e + 1)
                        if e == 0:
                            act.wait_ge(col_zero, n + 1)
                        nc.scalar.activation(xf[:, e, 1:BLK + 1], tps[e % 2][:], ACT.Copy).then_inc(xf_done, 1)
                        if e >= 1:
                            hi(e - 1)
                    hi(ET - 1)

                root(1)
                for n in range(6):
                    split_w(n)
                take_transposed(0)
                with act.Fori(0, B) as i:
                    for blk in range(NB):
                        n = i * NB + blk
                        tile0 = i * (NB * NT) + blk * NT
                        for m in range(2 * G):
                            c = blk * 2 * G + m
                            act.wait_ge(tile_done, tile0 + m + 1)
                            use = c // NS
                            act.wait_ge(stored[c % NS], i * (NB * 2 * G // NS * 32) + 32 * use + DMA_FIRST)
                            nc.scalar.activation(st_hi[c % NS][:], ring[(blk * NT + m) % RING][:], ACT.Copy
                                                 ).then_inc(st_hi_done, 1)
                            if m == 3:
                                act.wait_ge(mix_done, (n * 2 + 1) * ET)
                                nc.scalar.activation(b_hi[:], mix[:], ACT.Copy).then_inc(mhi_done, 1)
                        for t in range(TT):
                            c = blk * TT + t
                            act.wait_ge(tile_done, tile0 + V0 + t + 1)
                            act.wait_ge(v_stored[c % 2], i * (NB * TT // 2 * 16) + 16 * (c // 2) + DMA_FIRST)
                            nc.scalar.activation(v_st[c % 2][:], ring[(blk * NT + V0 + t) % RING][:], ACT.Copy)\
                                .then_inc(v_done, 1)
                        act.wait_ge(mix_done, (n * 2 + 2) * ET)
                        nc.scalar.activation(a_hi[:], mix[:], ACT.Copy).then_inc(mhi_done, 1)
                        root(n + 2)
                        for t in range(TT):
                            act.wait_ge(tile_done, tile0 + R0 + t + 1)
                            act.wait_ge(f_done, n * TT + FIRST)
                            nc.scalar.activation(gate[:, t, :], ring[(blk * NT + R0 + t) % RING][:], ACT.Tanh,
                                                 scale=0.5).then_inc(tanh_done, 1)

                        def key_hi(t):
                            act.wait_ge(sq_done, n * TT + t + 1)
                            nc.scalar.activation(b_hi[:, t, :], relu[t % 2][:], ACT.Copy).then_inc(chi_done, 1)
                        for t in range(TT):
                            act.wait_ge(tile_done, tile0 + C0 + t + 1)
                            if t >= 2:
                                act.wait_ge(clo_done, n * TT + t - 1 + FIRST)
                            else:
                                act.wait_ge(clo_done, n * TT + FIRST)
                            nc.scalar.activation(relu[t % 2][:], ring[(blk * NT + C0 + t) % RING][:], ACT.Relu)\
                                .then_inc(relu_done, 1)
                            if t >= 1:
                                key_hi(t - 1)
                        key_hi(TT - 1)
                        take_transposed(n + 1)

            @block.vector
            def _(dve):
                def split_w(n):
                    dve.wait_ge(w_split_hi, n + 1)
                    nc.vector.tensor_tensor(w_lo[n][:], (mix, gate)[n % 2][:], w_hi[n][:].bitcast(F32),
                                            ALU.subtract).then_inc(w_split, 1)

                def moments(buf, s, loads, n):
                    dve.wait_ge(x_ld[s], loads)
                    for t in range(TT):
                        nc.vector.bn_stats(stats[:, t, :], buf[:, t, :]).then_inc(stats_done, 1)
                    for t in range(TT):
                        dve.wait_ge(stats_done, n * TT + t + 1)
                        dve.nop(nofuse=True)
                        nc.vector.bn_aggr(mean_var[:, t, :], stats[:, t, :]).then_inc(aggr_done, 1)
                    dve.wait_ge(aggr_done, (n + 1) * TT)
                    nc.vector.tensor_scalar(var_eps[:], mean_var[:, :, 1], EPS, None, ALU.add).then_inc(var_done, 1)

                def normalise(buf, n):
                    dve.wait_ge(sd_done, n + 1)
                    nc.vector.reciprocal(rstd[:], sd[:]).then_inc(rstd_done, 1)
                    dve.wait_ge(rstd_done, n + 1)
                    for t in range(TT):
                        nc.vector.tensor_scalar(xn[:, t, :], buf[:, t, :], mean_var[:, t, 0:1], rstd[:, t:t + 1],
                                                ALU.subtract, ALU.mult).then_inc(xn_done, 1)

                def split_xn(n):
                    for e in range(ET):
                        dve.wait_ge(xhi_done, n * ET + e + 1)
                        nc.vector.tensor_tensor(a_lo[:, e, :], xf[:, e, 1:BLK + 1], a_hi[:, e, :].bitcast(F32),
                                                ALU.subtract).then_inc(xlo_done, 1)

                nc.vector.memset(xf[:, :, 0], 0.0).then_inc(col_zero, 1)
                moments(xb[0], 0, 16, 0)
                normalise(xb[0], 0)
                for n in range(6):
                    split_w(n)
                split_xn(0)
                dve.wait_ge(small_ld, 48)
                dve.wait_ge(col_zero, 1)
                with dve.Fori(0, B) as i:
                    for blk in range(NB):
                        n = i * NB + blk
                        tile0 = i * (NB * NT) + blk * NT

                        def split_tile(m):
                            c = blk * 2 * G + m
                            dve.wait_ge(st_hi_done, i * (NB * 2 * G) + c + 1)
                            nc.vector.tensor_tensor(st_lo[c % NS][:], ring[(blk * NT + m) % RING][:],
                                                    st_hi[c % NS][:].bitcast(F32), ALU.subtract).then_inc(qk_done, 1)

                        def mixed(which):
                            dve.wait_ge(step_done, n + 1)
                            for e in range(ET):
                                nc.vector.scalar_tensor_tensor(
                                    out=mix[:, e, :], in0=xn[:, e, :], scalar=mus[:, which, e:e + 1],
                                    in1=xf[:, e, 0:BLK], op0=ALU.mult, op1=ALU.add).then_inc(mix_done, 1)

                        def mix_lo(which, dst, hi):
                            dve.wait_ge(mhi_done, n * 2 + which + 1)
                            nc.vector.tensor_tensor(dst[:], mix[:], hi[:].bitcast(F32), ALU.subtract)\
                                .then_inc(mlo_done, 1)

                        split_tile(0)
                        dve.wait_ge(xf_done, (n + 1) * ET)
                        nc.vector.tensor_tensor(xn[:], xf[:, :, 1:BLK + 1], xf[:, :, 0:BLK], ALU.subtract)\
                            .then_inc(step_done, 1)
                        split_tile(1)
                        if blk == 0:
                            dve.wait_ge(mlo_done, n * 2 + FIRST)
                        mixed(0)
                        split_tile(2)
                        split_tile(3)
                        mix_lo(0, b_lo, b_hi)
                        split_tile(4)
                        dve.wait_ge(mlo_done, n * 2 + 1 + FIRST)
                        mixed(1)
                        split_tile(5)
                        dve.wait_ge(mix_done, (n * 2 + 2) * ET)
                        if blk < NB - 1:
                            nc.vector.tensor_copy(xf[:, :, 0:1], xf[:, :, BLK:BLK + 1]).then_inc(col_zero, 1)
                        else:
                            nc.vector.memset(xf[:, :, 0:1], 0.0).then_inc(col_zero, 1)
                        s = (blk + 1) % 2
                        moments(xb[s], s, i * 32 + (16 if s else 32) + 16 * ((blk - (1 - s)) // 2 if s else (blk - 1) // 2), n + 1)
                        split_tile(6)
                        split_tile(7)
                        normalise(xb[s], n + 1)
                        mix_lo(1, a_lo, a_hi)

                        def to_gate(t):
                            dve.wait_ge(tanh_done, n * TT + t + 1 + FIRST)
                            nc.vector.tensor_scalar(gate[:, t, :], gate[:, t, :], 0.5, 0.5, ALU.mult, ALU.add)\
                                .then_inc(gate_done, 1)

                        def key(t):
                            dve.wait_ge(relu_done, n * TT + t + 1 + FIRST)
                            nc.vector.tensor_tensor(relu[t % 2][:], relu[t % 2][:], relu[t % 2][:], ALU.mult)\
                                .then_inc(sq_done, 1)

                        def key_lo(t):
                            dve.wait_ge(chi_done, n * TT + t + 1)
                            nc.vector.tensor_tensor(b_lo[:, t, :], relu[t % 2][:], b_hi[:, t, :].bitcast(F32),
                                                    ALU.subtract).then_inc(clo_done, 1)

                        to_gate(0)
                        to_gate(1)
                        to_gate(2)
                        to_gate(3)
                        key(0)
                        key(1)
                        key_lo(0)
                        key(2)
                        key_lo(1)
                        key(3)
                        key_lo(2)
                        key_lo(3)
                        split_xn(n + 1)
                        dve.wait_ge(gate_done, (n + 1) * TT)
                        for t in range(TT):
                            c = blk * TT + t
                            dve.wait_ge(tile_done, tile0 + F0 + t + 1)
                            dve.wait_ge(part_stored[c % 2], i * (NB * TT // 2 * 16) + 16 * (c // 2) + DMA_FIRST)
                            nc.vector.tensor_tensor(f_out[c % 2][:], ring[(blk * NT + F0 + t) % RING][:],
                                                    gate[:, t, :], ALU.mult).then_inc(f_done, 1)

            @block.tensor
            def _(pe):
                def transposes(n, first=False):
                    pe.wait_ge(xn_done, (n + 1) * TT)
                    for e in range(ET):
                        if e >= 2:
                            pe.wait_ge(xf_done, n * ET + e - 1)
                        elif e == 0 and not first:
                            pe.wait_ge(xf_done, n * ET)
                        for t in range(TT):
                            last = nc.tensor.transpose(tps[e % 2][:, t * P:(t + 1) * P], xn[:, t, e * P:(e + 1) * P],
                                                       ident[:])
                        last.then_inc(t_done, 1)

                def product(n0, m, pairs, operand=None):
                    wait_ring(pe, n0, m)
                    out = ring[(n0[1] * NT + m) % RING]
                    for k, (lhs, rhs) in enumerate(pairs):
                        if operand and k % 3 == 0:
                            pe.wait_ge(operand[0], operand[1] + k // 3 + 1)
                        last = nc.tensor.matmul(out[:], lhs, rhs, start=(k == 0), stop=(k == len(pairs) - 1))
                    last.then_inc(tile_done, 1)

                def channels_out(a, w, cols):
                    return [(wx[:, e, cols], ax[:, e, :]) for e in range(ET)
                            for wx, ax in ((w_hi[w], a[0]), (w_hi[w], a[1]), (w_lo[w], a[0]))]

                def tokens_out(a, w, cols):
                    return [(ax[:, e, cols], wx[:, e, :]) for e in range(ET)
                            for ax, wx in ((a[0], w_hi[w]), (a[0], w_lo[w]), (a[1], w_hi[w]))]

                a, b = (a_hi, a_lo), (b_hi, b_lo)
                tile = [slice(t * P, (t + 1) * P) for t in range(4)]
                pe.wait_ge(ident_set, 1)
                transposes(0, first=True)
                pe.wait_ge(w_split, 6)
                with pe.Fori(0, B) as i:
                    for blk in range(NB):
                        n = i * NB + blk
                        n0 = (i, blk)
                        for g in range(G):
                            product(n0, Q0 + g, channels_out(a, 0, tile[g]), (xlo_done, n * ET) if g == 0 else None)
                        for g in range(G):
                            product(n0, K0 + g, channels_out(a, 1, tile[g]))
                        for t in range(TT):
                            product(n0, V0 + t, tokens_out(a, 2, tile[t]))
                        pe.wait_ge(mlo_done, n * 2 + 1 + FIRST)
                        for t in range(TT):
                            product(n0, R0 + t, tokens_out(b, 3, tile[t]))
                        pe.wait_ge(mlo_done, n * 2 + 2 + FIRST)
                        for t in range(TT):
                            product(n0, C0 + t, channels_out(a, 4, tile[t]))
                        transposes(n + 1)
                        for t in range(TT):
                            product(n0, F0 + t, tokens_out(b, 5, tile[t]),
                                    (clo_done, n * TT + FIRST) if t == 0 else None)


def attention(nc, q_hi, q_lo, k_hi, k_lo, v_all, ctx_t):
    NG = B * G
    KT = T // P
    STEPS = [TT * (j + 1) for j in range(NB)]
    S0 = [sum(STEPS[:j]) for j in range(NB)]
    NSTEP = sum(STEPS)
    NPAIR = NSTEP // 2
    NPR = 4
    NX = 3
    ENTRY = []
    for j in range(NB):
        chunks = [(j, h, r, c) for h in range(HG) for r in range(TT) for c in range(j + 1)]
        ENTRY += chunks[:2 * NX] + ([(j - 1,)] if j else []) + chunks[2 * NX:]
    ENTRY.append((NB - 1,))
    NENT = len(ENTRY)
    TAKEN = [sum(len(x) > 1 for x in ENTRY[:e + 1]) for e in range(NENT)]
    NTAKE = TAKEN[-1]
    AHEAD = 96
    ROWS_AHEAD = sum(len(x) == 1 for x in ENTRY[:AHEAD])

    def share_out():
        pe_work, dve_work = [], []
        for n in range(NSTEP):
            j = max(j for j in range(NB) if S0[j] <= n)
            r = n - S0[j] - j * TT
            w = BLK - max(r, 0) * P
            qk = (max(w, 2 * P) + (P if r >= 0 else 0)) / 2.4
            pe_work += [qk, qk, 4 * w / 2.4, qk, qk, 4 * w / 2.4 if n % 2 else 0]
            dve_work += [0] * 5 + [820 if 1 <= n - S0[j] <= TT else 0]
        cost = []
        for x in ENTRY[AHEAD:] + ENTRY[:AHEAD]:
            if len(x) == 1:
                cost.append(900 if x[0] == NB - 1 else 250)
            else:
                cost.append(80 + (BLK if x[3] < x[0] else (x[2] + 1) * P) / 0.96)
        rate = (sum(cost) + sum(dve_work)) / sum(pe_work)
        out, done, spare = [], 0, 0
        for a, b in zip(pe_work, dve_work):
            spare += a * rate - b
            until = done
            while until < NENT and cost[until] <= spare:
                spare -= cost[until]
                until += 1
            out.append((AHEAD + done, AHEAD + until))
            done = until
        out[-1] = (out[-1][0], AHEAD + NENT)
        return out

    SHARE = share_out()
    NPIECE = len(SHARE) // NSTEP

    def step(x):
        over, n = divmod(x, NSTEP)
        j = max(j for j in range(NB) if S0[j] <= n)
        return over, j, n - S0[j], n

    def unit_ended(x, last):
        over, j, kt, n = step(x)
        return over * NB + j if x >= 0 and kt == STEPS[j] - 1 and not (last and over == 2) else None

    PEEL = 6
    NPAIRS = NG // 2
    PAIR = 2 * NSTEP

    def entries_of(x, last):
        over, j, kt, n = step(x)
        pieces = [[(over + p // NENT, p % NENT) for p in range(*SHARE[n * NPIECE + k])] for k in range(NPIECE)]
        return [[x for x in piece if not (last and x[0] >= 2)] for piece in pieces]

    def bank(place, period):
        return place % period % NX

    def bank_before(place, period):
        at = place % period
        return place - NX if at >= NX else place - at - 1 - (period - 1 - at) % NX

    with ExitStack() as ctx:
        def sb(name, shape, dt=F32):
            return ctx.enter_context(nc.sbuf_tensor(name, shape, dt))

        def sem(name):
            return ctx.enter_context(nc.semaphore(name))

        qs = [sb(f"q_stack{s}", [P, HG, T], F32R) for s in range(2)]
        ks = [sb(f"k_stack{s}", [P, HG, T], F32R) for s in range(2)]
        vs = [sb(f"v_group{s}", [P, KT, P]) for s in range(2)]
        pr = [sb(f"probs{s}", [P, HG, BLK]) for s in range(NPR)]
        o_sb = [sb(f"o_sb{s}", [P, BLK]) for s in range(2)]
        s_sb = [sb(f"s_sb{s}", [P, BLK]) for s in range(2)]
        o_n = [sb(f"o_norm{s}", [P, BLK]) for s in range(2)]
        tri = sb("tri", [P, BLK])
        junk = [sb(f"junk{s}", [P, BLK]) for s in range(NX)]
        m_part = sb("m_part", [P, HG * TT, NB])
        m_neg = [sb(f"m_neg{s}", [P, HG * TT]) for s in range(2)]
        m_row = [sb(f"m_row{s}", [HG * TT, P], F32R) for s in range(2)]
        ident = sb("ident2", [P, P])
        ident_b = sb("ident_b", [P, P], BF16)
        tri_b = sb("tri_b", [P, P], BF16)
        ones = sb("ones", [P, HD])
        sT = [ctx.enter_context(nc.psum_tensor(f"scores_t{h}", [P, BLK], F32)) for h in range(NX)]
        mx = [ctx.enter_context(nc.psum_tensor(f"scores{s}", [P, BLK], F32)) for s in range(NX)]
        o_ps = ctx.enter_context(nc.psum_tensor("o_ps", [P, BLK], F32))
        s_ps = ctx.enter_context(nc.psum_tensor("s_ps", [P, BLK], F32))

        q_ld = [[sem(f"q_loaded{s}{j}") for j in range(NB)] for s in range(2)]
        kv_ld = [[sem(f"kv_loaded{s}{j}") for j in range(NB)] for s in range(2)]
        m_ld = [sem(f"m_loaded{j}") for j in range(NB)]
        o_st = [sem(f"o_stored{s}") for s in range(2)]
        cst0 = sem("const_base")
        cst = sem("const_ready")
        one_rows = sem("one_rows_ready")
        mm_done = sem("chunk_done")
        mx_freed = sem("chunk_taken")
        neg_done = sem("m_neg_ready")
        row_done = sem("m_row_ready")
        qk_done = sem("scores_t_done")
        ex_done = sem("probs_done")
        pv_done = sem("pv_done")
        pair_done = sem("pair_added")
        sm_done = sem("sum_done")
        o_cp = sem("o_copied")
        s_cp = sem("s_copied")
        rc_done = sem("recip_done")
        on_done = sem("o_norm_done")

        with nc.Block() as block:
            def load_q(sp, g, par, j):
                src = [a[bass.ds(g * P, P), j * BLK:(j + 1) * BLK].rearrange("(h d) t -> d h t", h=HG)
                       for a in (q_hi, q_hi, q_lo)]
                for c in range(3):
                    sp.dma_start(qs[par][c * HD:(c + 1) * HD, :, j * BLK:(j + 1) * BLK].bitcast(F32), src[c]
                                 ).then_inc(q_ld[par][j], 16)

            def load_kv(sp, g, par, j):
                src = [a[bass.ds(g * P, P), j * BLK:(j + 1) * BLK].rearrange("(h d) t -> d h t", h=HG)
                       for a in (k_hi, k_lo, k_hi)]
                for c in range(3):
                    sp.dma_start(ks[par][c * HD:(c + 1) * HD, :, j * BLK:(j + 1) * BLK].bitcast(F32), src[c]
                                 ).then_inc(kv_ld[par][j], 16)
                sp.dma_start(vs[par][:, j * TT:(j + 1) * TT, :],
                             v_all[bass.ds(g * T + j * BLK, BLK), :].rearrange("(t p) c -> p t c", p=P)
                             ).then_inc(kv_ld[par][j], 16)

            def store_m(sp, mg, par, j):
                u = j % 2
                sp.wait_ge(row_done, mg * NB + j + 1)
                for h in range(HG):
                    sp.dma_start(qs[par][QK_ROWS:QK_ROWS + 1, h, j * BLK:(j + 1) * BLK].bitcast(F32),
                                 m_row[u][h * TT:(h + 1) * TT, :].bitcast(F32)).then_inc(m_ld[j], 16)

            @block.sync
            def _(sp):
                start_counters(sp, [on_done], o_st)
                for j in range(NB):
                    load_kv(sp, 0, 0, j)
                    load_q(sp, 0, 0, j)
                for j in range(NB):
                    load_kv(sp, 1, 1, j)
                    load_q(sp, 1, 1, j)
                for j in range(ROWS_AHEAD):
                    store_m(sp, 0, 0, j)

                def store_o(g0, u):
                    par, j = divmod(u, NB)
                    sp.wait_ge(on_done, g0 * NB + u + 1 + FIRST)
                    sp.dma_start(ctx_t[bass.ds((g0 + par) * P, P), j * BLK:(j + 1) * BLK], o_n[u % 2][:]
                                 ).then_inc(o_st[u % 2], 16)

                def body(g0, last):
                    for par in range(2):
                        g = g0 + par
                        for j in range(NB):
                            u = par * NB + j
                            if not last:
                                if j == NB - 1:
                                    for c in range(NB - 1):
                                        sp.wait_ge(pv_done, g * NSTEP + S0[j] + (c + 1) * TT)
                                        load_kv(sp, g + 2, par, c)
                            if u >= 1:
                                store_o(g0, u - 1)
                            if j < NB - ROWS_AHEAD:
                                store_m(sp, g, par, ROWS_AHEAD + j)
                            elif not (last and par == 1):
                                store_m(sp, g + 1, 1 - par, j - (NB - ROWS_AHEAD))
                            if not last:
                                sp.wait_ge(qk_done, g * (NSTEP * HG) + (S0[j] + STEPS[j]) * HG)
                                load_q(sp, g + 2, par, j)
                        if not last:
                            sp.wait_ge(pv_done, (g + 1) * NSTEP)
                            load_kv(sp, g + 2, par, NB - 1)
                    store_o(g0, 2 * NB - 1)

                with sp.Fori(0, NPAIRS - 1) as i:
                    body(2 * i, False)
                body(NG - 2, True)
                for s in range(2):
                    sp.wait_ge(o_st[s], NG * NB // 2 * 16 + DMA_FIRST)

            @block.gpsimd
            def _(pool):
                nc.gpsimd.memset(ones[:], 1.0).then_inc(cst, 1)
                nc.gpsimd.memset(ident[:], 1.0).then_inc(cst0, 1)
                nc.gpsimd.memset(tri[:], 0.0).then_inc(cst0, 1)
                nc.gpsimd.memset(ident_b[:], 1.0).then_inc(cst0, 1)
                nc.gpsimd.memset(tri_b[:], 0.0).then_inc(cst0, 1)
                pool.wait_ge(cst0, 4)
                nc.gpsimd.affine_select(out=ident_b[:], in_=ident_b[:], compare_op=ALU.is_equal, fill=0.0, base=0,
                                        pattern=[[-1, P]], channel_multiplier=1).then_inc(cst, 1)
                nc.gpsimd.affine_select(out=tri_b[:], in_=tri_b[:], compare_op=ALU.is_ge, fill=MASKED, base=0,
                                        pattern=[[1, P]], channel_multiplier=-1).then_inc(cst, 1)
                nc.gpsimd.affine_select(out=ident[:], in_=ident[:], compare_op=ALU.is_equal, fill=0.0, base=0,
                                        pattern=[[-1, P]], channel_multiplier=1).then_inc(cst, 1)
                nc.gpsimd.affine_select(out=tri[:, BLK - P:BLK], in_=tri[:, BLK - P:BLK], compare_op=ALU.is_ge,
                                        fill=MASKED, base=0, pattern=[[-1, P]], channel_multiplier=1).then_inc(cst, 1)
                pool.wait_ge(cst, 5)
                for s in range(2):
                    nc.gpsimd.memset(ks[s][QK_ROWS:QK_ROWS + 1, :, :].bitcast(F32), 1.0).then_inc(one_rows, 1)
                pool.wait_ge(one_rows, 2)

                def at(g0, x, last):
                    over, j, kt, n = step(x)
                    g = g0 + over
                    if n % 2 == 1 and not (last and over == 2):
                        col = max(kt - j * TT, 0) * P
                        pool.wait_ge(ex_done, (g * NSTEP + n + 1) * HG)
                        pool.wait_ge(pv_done, g * NSTEP + n)
                        even, odd = pr[(x - 1) % NPR], pr[x % NPR]
                        nc.gpsimd.tensor_tensor(even[:, :, col:], even[:, :, col:], odd[:, :, col:], ALU.add)\
                            .then_inc(pair_done, 1)
                    u = unit_ended(x - 6, last)
                    if u is not None:
                        pool.wait_ge(rc_done, (g0 * NB + u + 1) * TT)
                        pool.wait_ge(o_st[u % 2], (g0 * NB + u - u % 2) * 8 + DMA_FIRST)
                        nc.gpsimd.tensor_tensor(o_n[u % 2][:], o_sb[u % 2][:], s_sb[u % 2][:], ALU.mult)\
                            .then_inc(on_done, 1)

                for x in range(PEEL):
                    at(0, x, False)
                with pool.Fori(0, NPAIRS - 1) as i:
                    for x in range(PEEL, PAIR + PEEL):
                        at(2 * i, x, False)
                for x in range(PEEL, PAIR + PEEL):
                    at(NG - 2, x, True)

            @block.scalar
            def _(act):
                def at(g0, x, last):
                    over, j, kt, n = step(x)
                    g = g0 + over
                    if not (last and over == 2):
                        col = max(kt - j * TT, 0) * P
                        if x >= NPR:
                            act.wait_ge(sm_done, g0 * NPAIR + (x - NPR) // 2 + 1)
                        for h in range(HG):
                            act.wait_ge(qk_done, (g * NSTEP + n) * HG + h + 1)
                            nc.scalar.activation(pr[x % NPR][:, h, col:], sT[bank(x * HG + h, PAIR * HG)][:, col:],
                                                 ACT.Exp, scale=SCALE).then_inc(ex_done, 1)
                    u = unit_ended(x - 1, last)
                    if u is not None:
                        act.wait_ge(on_done, g0 * NB + max(u - 1, 0) + FIRST)
                        act.wait_ge(pv_done, g0 * NSTEP + x)
                        nc.scalar.activation(o_sb[u % 2][:], o_ps[:], ACT.Copy).then_inc(o_cp, 1)
                    u = unit_ended(x - 2, last)
                    if u is not None:
                        act.wait_ge(sm_done, g0 * NPAIR + (x - 1) // 2)
                        nc.scalar.activation(s_sb[u % 2][:], s_ps[:], ACT.Copy).then_inc(s_cp, 1)

                for x in range(PEEL):
                    at(0, x, False)
                with act.Fori(0, NPAIRS - 1) as i:
                    for x in range(PEEL, PAIR + PEEL):
                        at(2 * i, x, False)
                for x in range(PEEL, PAIR + PEEL):
                    at(NG - 2, x, True)

            @block.vector
            def _(dve):
                dve.wait_ge(cst, 5)

                def take(mg0, over, e, first=False):
                    mg = mg0 + over
                    s = bank(over * NENT + e - AHEAD, 2 * NENT)
                    dve.wait_ge(mm_done, mg * NENT + e + 1)
                    if len(ENTRY[e]) == 1:
                        j, = ENTRY[e]
                        if j >= 2:
                            dve.wait_ge(m_ld[j - 2], (mg + 1) * (HG * 16))
                        elif not first:
                            dve.wait_ge(m_ld[j + 2], mg * (HG * 16))
                        nc.vector.tensor_copy(m_row[j % 2][:], mx[s][0:HG * TT, 0:P]).then_inc(row_done, 1)
                        return
                    j, h, r, c = ENTRY[e]
                    if (h, r, c) == (0, 0, 0) and not (first and j == 0):
                        dve.wait_ge(neg_done, mg * NB + j)
                    dst = m_part[:, h * TT + r, c:c + 1]
                    if c < j:
                        nc.vector.tensor_reduce(dst, mx[s][:], AX_X, ALU.max).then_inc(mx_freed, 1)
                    else:
                        w = (r + 1) * P
                        dve.nop(nofuse=True)
                        nc.vector.tensor_tensor_reduce(
                            out=junk[s][:, 0:w], in0=mx[s][:, 0:w], in1=tri[:, BLK - w:BLK], scale=1.0,
                            scalar=MASKED, op0=ALU.add, op1=ALU.max, accum_out=dst).then_inc(mx_freed, 1)
                    if (h, r, c) == (HG - 1, TT - 1, j):
                        dve.wait_ge(mx_freed, mg * NTAKE + TAKEN[e])
                        nc.vector.tensor_reduce(m_neg[j % 2][:], m_part[:, :, 0:j + 1], AX_X, ALU.max,
                                                negate=True).then_inc(neg_done, 1)

                for e in range(AHEAD):
                    take(0, 0, e, first=True)

                def at(g0, x, last):
                    for piece in entries_of(x, last):
                        for over, e in piece:
                            take(g0, over, e)
                    for piece in range(TT):
                        u = unit_ended(x - 2 - piece, last)
                        if u is not None:
                            dve.wait_ge(s_cp, g0 * NB + u + 1)
                            sums = s_sb[u % 2][:, piece * P:(piece + 1) * P]
                            nc.vector.reciprocal(sums, sums).then_inc(rc_done, 1)

                for x in range(PEEL):
                    at(0, x, False)
                with dve.Fori(0, NPAIRS - 1) as i:
                    for x in range(PEEL, PAIR + PEEL):
                        at(2 * i, x, False)
                for x in range(PEEL, PAIR + PEEL):
                    at(NG - 2, x, True)

            @block.tensor
            def _(pe):
                pe.wait_ge(cst, 5)

                def entry(i, over, e, first=False):
                    mpar, mg = over % 2, 2 * i + over
                    place = over * NENT + e - AHEAD
                    dst = mx[bank(place, 2 * NENT)]
                    if not (first and e < NX):
                        og, oe = divmod(bank_before(place, 2 * NENT) + AHEAD, NENT)
                        if len(ENTRY[oe]) == 1:
                            pe.wait_ge(row_done, (2 * i + og) * NB + ENTRY[oe][0] + 1)
                        else:
                            pe.wait_ge(mx_freed, (2 * i + og) * NTAKE + TAKEN[oe])
                    if len(ENTRY[e]) == 1:
                        j, = ENTRY[e]
                        pe.wait_ge(neg_done, mg * NB + j + 1)
                        nc.tensor.transpose(dst[0:HG * TT, 0:P], m_neg[j % 2][:], ident[:]).then_inc(mm_done, 1)
                        return
                    j, h, r, c = ENTRY[e]
                    if (h, r, c) == (0, 0, 0):
                        pe.wait_ge(kv_ld[mpar][j], (i + over // 2 + 1) * 64)
                        pe.wait_ge(q_ld[mpar][j], (i + over // 2 + 1) * 48)
                    w = BLK if c < j else max((r + 1) * P, 2 * P)
                    q0 = j * BLK + r * P
                    nc.tensor.matmul(dst[:, 0:w], qs[mpar][0:QK_ROWS, h, q0:q0 + P],
                                     ks[mpar][0:QK_ROWS, h, c * BLK:c * BLK + w], start=True, stop=True)\
                        .then_inc(mm_done, 1)

                def scores(g0, x, h):
                    over, j, kt, n = step(x)
                    par = over % 2
                    q = x * HG + h
                    dst = sT[bank(q, PAIR * HG)]
                    if kt == 0 and h == 0:
                        pe.wait_ge(m_ld[j], (g0 + over + 1) * (HG * 16))
                    if q >= NX:
                        pe.wait_ge(ex_done, g0 * (NSTEP * HG) + bank_before(q, PAIR * HG) + 1)
                    col = min(max(kt - j * TT, 0) * P, BLK - 2 * P)
                    last = nc.tensor.matmul(dst[:, col:], ks[par][0:QK_ROWS + 1, h, kt * P:(kt + 1) * P],
                                            qs[par][0:QK_ROWS + 1, h, j * BLK + col:(j + 1) * BLK],
                                            start=True, stop=True)
                    if kt >= j * TT:
                        d = (kt - j * TT) * P
                        last = nc.tensor.matmul(dst[:, d:d + P], ident_b[:], tri_b[:], start=False, stop=True,
                                                skip_group_check=True)
                    last.then_inc(qk_done, 1)

                def side_by_side(dst, x, lhs):
                    over, j, kt, n = step(x)
                    col = max(kt - j * TT, 0) * P
                    for h in range(HG):
                        last = nc.tensor.matmul(dst[h * HD:(h + 1) * HD, col:], lhs[h], pr[x % NPR][:, h, col:],
                                                start=(kt == 0), stop=(kt >= STEPS[j] - (1 if dst is o_ps else 2)))
                    return last

                def weigh(g0, x):
                    over, j, kt, n = step(x)
                    pe.wait_ge(ex_done, (g0 * NSTEP + x + 1) * HG)
                    if kt == 0 and x > 0:
                        pe.wait_ge(o_cp, (g0 + over) * NB + j)
                    side_by_side(o_ps, x, [vs[over % 2][:, kt, h * HD:(h + 1) * HD] for h in range(HG)])\
                        .then_inc(pv_done, 1)

                def total(g0, x):
                    over, j, kt, n = step(x)
                    if kt == 0 and x > 0:
                        pe.wait_ge(s_cp, (g0 + over) * NB + j)
                    pe.wait_ge(pair_done, g0 * NPAIR + x // 2 + 1)
                    side_by_side(s_ps, x, [ones[:]] * HG).then_inc(sm_done, 1)

                def at(i, g0, x, last):
                    entries = entries_of(x, last)

                    def begin(piece):
                        for over, e in entries[piece]:
                            entry(i, over, e)

                    live = not (last and x >= PAIR)
                    if live:
                        scores(g0, x, 0)
                        begin(0)
                        scores(g0, x, 1)
                        begin(1)
                    if x >= 1 and not (last and x > PAIR):
                        weigh(g0, x - 1)
                    if live:
                        begin(2)
                        scores(g0, x, 2)
                        begin(3)
                        scores(g0, x, 3)
                        begin(4)
                    if x >= 3 and x % 2 == 1 and not (last and x - 3 >= PAIR):
                        total(g0, x - 3)
                    if live:
                        begin(5)

                for e in range(AHEAD):
                    entry(0, 0, e, first=True)
                pe.wait_ge(one_rows, 2)
                for x in range(PEEL):
                    at(0, 0, x, False)
                with pe.Fori(0, NPAIRS - 1) as i:
                    for x in range(PEEL, PAIR + PEEL):
                        at(i, 2 * i, x, False)
                for x in range(PEEL, PAIR + PEEL):
                    at(NPAIRS - 1, NG - 2, x, True)


def project_out(nc, ctx_t, w_o, part, out):
    NBLK = B * NB
    with ExitStack() as ctx:
        def sb(name, shape, dt=F32):
            return ctx.enter_context(nc.sbuf_tensor(name, shape, dt))

        def sem(name):
            return ctx.enter_context(nc.semaphore(name))

        w_raw = sb("wo_raw", [P, ET, D])
        w_hi = sb("wo_hi", [P, ET, D], F32R)
        w_lo = sb("wo_lo", [P, ET, D], F32R)
        c_raw = [sb(f"ctx{s}", [P, ET, BLK]) for s in range(2)]
        c_hi = [sb(f"ctx_hi{s}", [P, ET, BLK], F32R) for s in range(2)]
        c_lo = [sb(f"ctx_lo{s}", [P, ET, BLK], F32R) for s in range(2)]
        res = [sb(f"res{s}", [P, TT, D]) for s in range(2)]
        ps = [ctx.enter_context(nc.psum_tensor(f"out_ps{s}", [P, D], F32)) for s in range(2 * TT)]
        w_ld = sem("wo_loaded")
        whi = sem("wo_hi_ready")
        wlo = sem("wo_lo_ready")
        c_ld = [sem(f"ctx_loaded{s}") for s in range(2)]
        r_ld = [sem(f"res_loaded{s}") for s in range(2)]
        chi = sem("ctx_hi_ready")
        clo = sem("ctx_lo_ready")
        done = sem("out_tile_done")
        added = sem("out_added")
        stored = [sem(f"out_stored{s}") for s in range(2)]

        with nc.Block() as block:
            @block.sync
            def _(sp):
                start_counters(sp, [clo, done, added], stored)
                sp.dma_start(w_raw[:], w_o.rearrange("(t p) a -> p t a", p=P)).then_inc(w_ld, 16)
                with sp.Fori(0, B) as i:
                    for j in range(NB):
                        s = j % 2
                        n = i * NB + j
                        half = i * (NB // 2) + j // 2
                        if j >= 2:
                            sp.wait_ge(clo, n - 1 + FIRST)
                        else:
                            sp.wait_ge(clo, i * NB + FIRST)
                        sp.dma_start(c_raw[s][:], ctx_t[bass.ds(i * (G * P), G * P), j * BLK:(j + 1) * BLK]
                                     .rearrange("(g p) t -> p g t", p=P)).then_inc(c_ld[s], 16)
                        sp.wait_ge(stored[s], half * 16 + DMA_FIRST)
                        sp.dma_start(res[s][:], part[bass.ds(i * T + j * BLK, BLK), :]
                                     .rearrange("(t p) d -> p t d", p=P)).then_inc(r_ld[s], 16)
                for s in range(2):
                    sp.wait_ge(stored[s], NBLK // 2 * 16 + DMA_FIRST)

            @block.scalar
            def _(act):
                act.wait_ge(w_ld, 16)
                nc.scalar.activation(w_hi[:], w_raw[:], ACT.Copy).then_inc(whi, 1)
                with act.Fori(0, B) as i:
                    for j in range(NB):
                        s = j % 2
                        n = i * NB + j
                        half = i * (NB // 2) + j // 2
                        act.wait_ge(c_ld[s], half * 16 + 16)
                        act.wait_ge(done, (i * NB + max(j - 1, 0)) * TT + FIRST)
                        nc.scalar.activation(c_hi[s][:], c_raw[s][:], ACT.Copy).then_inc(chi, 1)
                        if j >= 1:
                            act.wait_ge(added, n * TT + FIRST)
                            act.dma_start(out[bass.ds(i * T + (j - 1) * BLK, BLK), :]
                                          .rearrange("(t p) d -> p t d", p=P), res[1 - s][:]).then_inc(stored[1 - s], 16)
                    act.wait_ge(added, (i + 1) * (NB * TT) + FIRST)
                    act.dma_start(out[bass.ds(i * T + (NB - 1) * BLK, BLK), :]
                                  .rearrange("(t p) d -> p t d", p=P), res[1][:]).then_inc(stored[1], 16)

            @block.gpsimd
            def _(pool):
                with pool.Fori(0, B) as i:
                    for j in range(NB):
                        s = j % 2
                        pool.wait_ge(chi, i * NB + j + 1)
                        nc.gpsimd.tensor_tensor(c_lo[s][:], c_raw[s][:], c_hi[s][:].bitcast(F32), ALU.subtract)\
                            .then_inc(clo, 1)

            @block.vector
            def _(dve):
                dve.wait_ge(whi, 1)
                nc.vector.tensor_tensor(w_lo[:], w_raw[:], w_hi[:].bitcast(F32), ALU.subtract).then_inc(wlo, 1)

                with dve.Fori(0, B) as i:
                    for j in range(NB):
                        s = j % 2
                        n = i * NB + j
                        half = i * (NB // 2) + j // 2
                        dve.wait_ge(r_ld[s], half * 16 + 16)
                        for t in range(TT):
                            dve.wait_ge(done, n * TT + t + 1 + FIRST)
                            nc.vector.tensor_tensor(res[s][:, t, :], ps[s * TT + t][:], res[s][:, t, :], ALU.add)\
                                .then_inc(added, 1)

            @block.tensor
            def _(pe):
                pe.wait_ge(wlo, 1)
                with pe.Fori(0, B) as i:
                    for j in range(NB):
                        s = j % 2
                        n = i * NB + j
                        pe.wait_ge(clo, n + 1 + FIRST)
                        pe.wait_ge(added, (i * NB + max(j - 1, 0)) * TT + FIRST)
                        for t in range(TT):
                            pairs = [(ax[:, e, t * P:(t + 1) * P], wx[:, e, :]) for e in range(ET)
                                     for ax, wx in ((c_hi[s], w_hi), (c_hi[s], w_lo), (c_lo[s], w_hi))]
                            for k, (lhs, rhs) in enumerate(pairs):
                                last = nc.tensor.matmul(ps[s * TT + t][:], lhs, rhs, start=(k == 0),
                                                        stop=(k == len(pairs) - 1))
                            last.then_inc(done, 1)


def build_program(nc, x, w_t, w_o, b_o, mu_r, mu_k, out):
    def scratch(name, shape, dt=F32):
        return nc.dram_tensor(name, shape, dt, kind="Internal").ap()

    split = [scratch(n, [B * G * P, T]) for n in ("q_hi", "q_lo", "k_hi", "k_lo")]
    v_all = scratch("v_all", [B * G * T, P])
    part = scratch("part", [B * T, D])
    ctx_t = scratch("ctx_t", [B * G * P, T])
    project_and_ffn(nc, x, w_t, b_o, mu_r, mu_k, *split, v_all, part)
    attention(nc, *split, v_all, ctx_t)
    project_out(nc, ctx_t, w_o, part, out)


def kernel(**inputs):
    import numpy as _np
    import concourse.bacc as _bacc
    from concourse import mybir as _mybir
    from concourse.bass_utils import run_bass_kernel_spmd as _run

    nc = _bacc.Bacc("TRN2", target_bir_lowering=False, num_devices=1)
    nc.disable_value_cache = True
    a = {k: _np.asarray(v) for k, v in inputs.items()}
    laid = {
        "x": a["L0_attn_x"].reshape(B * T, D),
        "b_o": _np.broadcast_to(a["L0_attn_b_o"], (P, D)),
        "mu_r": a["L0_ffn_mu_r"].reshape(ET, P).T,
        "mu_k": a["L0_ffn_mu_k"].reshape(ET, P).T,
    }
    names = ["L0_attn_W_q", "L0_attn_W_k", "L0_attn_W_v", "L0_ffn_W_r", "L0_ffn_W_k", "L0_ffn_W_v", "L0_attn_W_o"]
    for n, name in enumerate(names):
        laid[f"w{n}"] = a[name].T
    laid = {k: _np.ascontiguousarray(v) for k, v in laid.items()}
    h = {k: nc.dram_tensor(f"in_{k}", v.shape, _mybir.dt.from_np(v.dtype), kind="ExternalInput").ap()
         for k, v in laid.items()}
    out = nc.dram_tensor("out_0", (B * T, D), _mybir.dt.float32, kind="ExternalOutput").ap()
    build_program(nc, h["x"], [h[f"w{n}"] for n in range(6)], h["w6"], h["b_o"], h["mu_r"], h["mu_k"], out)
    r = _run(nc, [{f"in_{k}": v for k, v in laid.items()}], core_ids=[0])
    return r.results[0]["out_0"].reshape(B, T, D)
```

```python
from contextlib import ExitStack

import concourse.bass as bass
from concourse import mybir

F32 = mybir.dt.float32
F32R = mybir.dt.float32r
BF16 = mybir.dt.bfloat16
ALU = mybir.AluOpType
ACT = mybir.ActivationFunctionType
AX_X = mybir.AxisListType.X

P = 128
B, T, D = 4, 2048, 512
H, HD = 16, 32
HG = P // HD
G = H // HG
BLK = 512
NB = T // BLK
ET = D // P
TT = BLK // P
QK_ROWS = 3 * HD
SCALE = float(HD) ** -0.5
EPS = 1e-5
MASKED = -1e30

FIRST = 1
DMA_FIRST = 16



def start_counters(eng, counters, dma_counters):
    for c in counters:
        eng.sem_inc(c, FIRST)
    for c in dma_counters:
        eng.sem_inc(c, DMA_FIRST)


def project_and_ffn(nc, x, w_t, b_o, mu_r, mu_k, q_hi, q_lo, k_hi, k_lo, v_all, part):
    NT = 2 * G + 4 * TT
    RING = 6
    Q0, K0, V0, R0, C0, F0 = 0, G, 2 * G, 2 * G + TT, 2 * G + 2 * TT, 2 * G + 3 * TT
    NS = 4
    with ExitStack() as ctx:
        def sb(name, shape, dt=F32):
            return ctx.enter_context(nc.sbuf_tensor(name, shape, dt))

        def sem(name):
            return ctx.enter_context(nc.semaphore(name))

        w_hi = [sb(f"w_hi{n}", [P, ET, D], F32R) for n in range(6)]
        w_lo = [sb(f"w_lo{n}", [P, ET, D], F32R) for n in range(6)]
        xb = [sb(f"x_block{s}", [P, TT, D]) for s in range(2)]
        xn = sb("xn", [P, TT, D])
        xf = sb("xn_t", [P, ET, BLK + 1])
        mix = sb("mix", [P, ET, BLK])
        a_hi = sb("a_hi", [P, ET, BLK], F32R)
        a_lo = sb("a_lo", [P, ET, BLK], F32R)
        b_hi = sb("b_hi", [P, ET, BLK], F32R)
        b_lo = sb("b_lo", [P, ET, BLK], F32R)
        st_hi = [sb(f"st_hi{s}", [P, BLK], F32R) for s in range(NS)]
        st_lo = [sb(f"st_lo{s}", [P, BLK], F32R) for s in range(NS)]
        v_st = [sb(f"v_st{s}", [P, D]) for s in range(2)]
        gate = sb("gate", [P, TT, D])
        relu = [sb(f"relu{s}", [P, BLK]) for s in range(2)]
        f_out = [sb(f"f_out{s}", [P, D]) for s in range(2)]
        bias = sb("bias", [P, D])
        mus = sb("mus", [P, 2, ET])
        ident = sb("ident", [P, P])
        stats = sb("stats", [P, TT, 6])
        mean_var = sb("mean_var", [P, TT, 2])
        var_eps = sb("var_eps", [P, TT])
        sd = sb("sd", [P, TT])
        rstd = sb("rstd", [P, TT])
        ring = [ctx.enter_context(nc.psum_tensor(f"ring{s}", [P, BLK], F32)) for s in range(RING)]
        tps = [ctx.enter_context(nc.psum_tensor(f"tps{s}", [P, BLK], F32)) for s in range(2)]

        w_in = [mix[:], gate[:], xb[1][:]]
        NW = len(w_in)
        w_ld = [sem(f"w_loaded{s}") for s in range(NW)]
        w_split_hi = sem("w_split_hi")
        w_split = sem("w_split")
        small_ld = sem("small_loaded")
        x_ld = [sem(f"x_loaded{s}") for s in range(2)]
        ones_set = sem("ones_set")
        ident_set = sem("ident_set")
        stats_done = sem("stats_done")
        aggr_done = sem("aggr_done")
        var_done = sem("var_done")
        sd_done = sem("sd_done")
        rstd_done = sem("rstd_done")
        xn_done = sem("xn_done")
        res_done = sem("residual_done")
        t_done = sem("transposed")
        xf_done = sem("xn_t_ready")
        xhi_done = sem("xn_hi_ready")
        xlo_done = sem("xn_lo_ready")
        col_zero = sem("column0_ready")
        step_done = sem("step_ready")
        mix_done = sem("mix_ready")
        mhi_done = sem("mix_hi_ready")
        mlo_done = sem("mix_lo_ready")
        tile_done = sem("tile_done")
        qk_done = sem("qk_split")
        st_hi_done = sem("stage_hi")
        stored = [sem(f"stage_stored{s}") for s in range(NS)]
        v_done = sem("v_done")
        v_stored = [sem(f"v_stored{s}") for s in range(2)]
        tanh_done = sem("tanh_done")
        gate_done = sem("gate_done")
        relu_done = sem("relu_done")
        sq_done = sem("square_done")
        chi_done = sem("key_hi_ready")
        clo_done = sem("key_lo_ready")
        f_done = sem("f_done")
        part_done = sem("part_done")
        part_stored = [sem(f"part_stored{s}") for s in range(2)]

        LAST_READER = [(qk_done, Q0, 2 * G), (v_done, V0, TT), (tanh_done, R0, TT), (relu_done, C0, TT),
                       (f_done, F0, TT)]

        def wait_ring(eng, n0, m):
            i, blk = n0
            prev = blk * NT + m - RING
            for done, first, count in LAST_READER:
                if prev < 0:
                    eng.wait_ge(done, i * (NB * count) + FIRST)
                elif first <= prev % NT < first + count:
                    eng.wait_ge(done, i * (NB * count) + prev // NT * count + prev % NT - first + 1 + FIRST)

        with nc.Block() as block:
            @block.sync
            def _(sp):
                start_counters(sp, [qk_done, v_done, tanh_done, relu_done, f_done, clo_done, mlo_done],
                               stored + v_stored + part_stored)
                sp.dma_start(xb[0][:], x[0:BLK, :].rearrange("(t p) d -> p t d", p=P)).then_inc(x_ld[0], 16)
                sp.dma_start(bias[:], b_o).then_inc(small_ld, 16)
                sp.dma_start(mus[:, 0, :], mu_r).then_inc(small_ld, 16)
                sp.dma_start(mus[:, 1, :], mu_k).then_inc(small_ld, 16)
                for n in range(6):
                    if n >= NW:
                        sp.wait_ge(w_split, n - NW + 1)
                    sp.dma_start(w_in[n % NW], w_t[n].rearrange("(t p) a -> p t a", p=P)).then_inc(w_ld[n % NW], 16)
                with sp.Fori(0, B) as i:
                    for blk in range(NB):
                        for m in range(2 * G):
                            if m == K0:
                                sp.wait_ge(w_split, 6)
                                row = i * T + (blk + 1) * BLK if blk < NB - 1 else ((i + 1) % B) * T
                                sp.dma_start(xb[(blk + 1) % 2][:],
                                             x[bass.ds(row, BLK), :].rearrange("(t p) d -> p t d", p=P)
                                             ).then_inc(x_ld[(blk + 1) % 2], 16)
                            c = blk * 2 * G + m
                            g = m % G
                            hi, lo = (q_hi, q_lo) if m < K0 else (k_hi, k_lo)
                            rows = bass.ds(i * (G * P) + g * P, P)
                            sp.wait_ge(qk_done, i * (NB * 2 * G) + c + 1 + FIRST)
                            for dst, src in ((hi, st_hi), (lo, st_lo)):
                                sp.dma_start(dst[rows, blk * BLK:(blk + 1) * BLK], src[c % NS][:].bitcast(F32)
                                             ).then_inc(stored[c % NS], 16)
                        for t in range(TT):
                            c = blk * TT + t
                            sp.wait_ge(v_done, i * (NB * TT) + c + 1 + FIRST)
                            dst = v_all[bass.ds(i * (G * T), G * T), :].rearrange("(g t) c -> t g c", g=G)
                            sp.dma_start(dst[c * P:(c + 1) * P, :, :],
                                         v_st[c % 2][:].rearrange("p (g c) -> p g c", g=G)
                                         ).then_inc(v_stored[c % 2], 16)
                        for t in range(TT):
                            c = blk * TT + t
                            sp.wait_ge(part_done, i * (NB * TT) + c + 1)
                            sp.dma_start(part[bass.ds(i * T + c * P, P), :], f_out[c % 2][:]
                                         ).then_inc(part_stored[c % 2], 16)
                for s in range(2):
                    sp.wait_ge(x_ld[s], 16 * (B * NB // 2 + 1 - s))
                for s in range(NS):
                    sp.wait_ge(stored[s], B * NB * 2 * G // NS * 32 + DMA_FIRST)
                for s in range(2):
                    sp.wait_ge(v_stored[s], B * NB * TT // 2 * 16 + DMA_FIRST)
                    sp.wait_ge(part_stored[s], B * NB * TT // 2 * 16 + DMA_FIRST)

            @block.gpsimd
            def _(pool):
                nc.gpsimd.memset(ident[:], 1.0).then_inc(ones_set, 1)
                pool.wait_ge(ones_set, 1)
                nc.gpsimd.affine_select(out=ident[:], in_=ident[:], compare_op=ALU.is_equal, fill=0.0, base=0,
                                        pattern=[[-1, P]], channel_multiplier=1).then_inc(ident_set, 1)
                pool.wait_ge(small_ld, 48)

                def residual(buf, n):
                    pool.wait_ge(xn_done, n)
                    for t in range(TT):
                        nc.gpsimd.tensor_tensor(buf[:, t, :], buf[:, t, :], bias[:], ALU.add).then_inc(res_done, 1)

                residual(xb[0], TT)
                with pool.Fori(0, B) as i:
                    for blk in range(NB):
                        n = i * NB + blk
                        residual(xb[(blk + 1) % 2], (n + 2) * TT)
                        for t in range(TT):
                            c = blk * TT + t
                            pool.wait_ge(f_done, i * (NB * TT) + c + 1 + FIRST)
                            pool.wait_ge(res_done, (n + 1) * TT)
                            nc.gpsimd.tensor_tensor(f_out[c % 2][:], f_out[c % 2][:], xb[blk % 2][:, t, :],
                                                    ALU.add).then_inc(part_done, 1)

            @block.scalar
            def _(act):
                def split_w(n):
                    act.wait_ge(w_ld[n % NW], 16 * (n // NW + 1))
                    nc.scalar.activation(w_hi[n][:], w_in[n % NW], ACT.Copy).then_inc(w_split_hi, 1)

                def root(n):
                    act.wait_ge(var_done, n)
                    nc.scalar.activation(sd[:], var_eps[:], ACT.Sqrt).then_inc(sd_done, 1)

                def take_transposed(n):
                    def hi(e):
                        act.wait_ge(xf_done, n * ET + e + 1)
                        nc.scalar.activation(a_hi[:, e, :], xf[:, e, 1:BLK + 1], ACT.Copy).then_inc(xhi_done, 1)
                    for e in range(ET):
                        act.wait_ge(t_done, n * ET + e + 1)
                        if e == 0:
                            act.wait_ge(col_zero, n + 1)
                        nc.scalar.activation(xf[:, e, 1:BLK + 1], tps[e % 2][:], ACT.Copy).then_inc(xf_done, 1)
                        if e >= 1:
                            hi(e - 1)
                    hi(ET - 1)

                root(1)
                split_w(0)
                take_transposed(0)
                for n in range(1, 6):
                    split_w(n)
                with act.Fori(0, B) as i:
                    for blk in range(NB):
                        n = i * NB + blk
                        tile0 = i * (NB * NT) + blk * NT
                        for m in range(2 * G):
                            c = blk * 2 * G + m
                            act.wait_ge(tile_done, tile0 + m + 1)
                            use = c // NS
                            act.wait_ge(stored[c % NS], i * (NB * 2 * G // NS * 32) + 32 * use + DMA_FIRST)
                            nc.scalar.activation(st_hi[c % NS][:], ring[(blk * NT + m) % RING][:], ACT.Copy
                                                 ).then_inc(st_hi_done, 1)
                            if m == 3:
                                act.wait_ge(mix_done, (n * 2 + 1) * ET)
                                nc.scalar.activation(b_hi[:], mix[:], ACT.Copy).then_inc(mhi_done, 1)
                        for t in range(TT):
                            c = blk * TT + t
                            act.wait_ge(tile_done, tile0 + V0 + t + 1)
                            act.wait_ge(v_stored[c % 2], i * (NB * TT // 2 * 16) + 16 * (c // 2) + DMA_FIRST)
                            nc.scalar.activation(v_st[c % 2][:], ring[(blk * NT + V0 + t) % RING][:], ACT.Copy)\
                                .then_inc(v_done, 1)
                        act.wait_ge(mix_done, (n * 2 + 2) * ET)
                        nc.scalar.activation(a_hi[:], mix[:], ACT.Copy).then_inc(mhi_done, 1)
                        root(n + 2)
                        for t in range(TT):
                            act.wait_ge(tile_done, tile0 + R0 + t + 1)
                            act.wait_ge(f_done, n * TT + FIRST)
                            nc.scalar.activation(gate[:, t, :], ring[(blk * NT + R0 + t) % RING][:], ACT.Tanh,
                                                 scale=0.5).then_inc(tanh_done, 1)

                        def key_hi(t):
                            act.wait_ge(sq_done, n * TT + t + 1)
                            nc.scalar.activation(b_hi[:, t, :], relu[t % 2][:], ACT.Copy).then_inc(chi_done, 1)
                        for t in range(TT):
                            act.wait_ge(tile_done, tile0 + C0 + t + 1)
                            if t >= 2:
                                act.wait_ge(clo_done, n * TT + t - 1 + FIRST)
                            else:
                                act.wait_ge(clo_done, n * TT + FIRST)
                            nc.scalar.activation(relu[t % 2][:], ring[(blk * NT + C0 + t) % RING][:], ACT.Relu)\
                                .then_inc(relu_done, 1)
                            if t >= 1:
                                key_hi(t - 1)
                        key_hi(TT - 1)
                        take_transposed(n + 1)

            @block.vector
            def _(dve):
                def split_w(n):
                    dve.wait_ge(w_split_hi, n + 1)
                    nc.vector.tensor_tensor(w_lo[n][:], w_in[n % NW], w_hi[n][:].bitcast(F32),
                                            ALU.subtract).then_inc(w_split, 1)

                def moments(buf, s, loads, n):
                    dve.wait_ge(x_ld[s], loads)
                    for t in range(TT):
                        nc.vector.bn_stats(stats[:, t, :], buf[:, t, :]).then_inc(stats_done, 1)
                    for t in range(TT):
                        dve.wait_ge(stats_done, n * TT + t + 1)
                        dve.nop(nofuse=True)
                        nc.vector.bn_aggr(mean_var[:, t, :], stats[:, t, :]).then_inc(aggr_done, 1)
                    dve.wait_ge(aggr_done, (n + 1) * TT)
                    nc.vector.tensor_scalar(var_eps[:], mean_var[:, :, 1], EPS, None, ALU.add).then_inc(var_done, 1)

                def normalise(buf, n):
                    dve.wait_ge(sd_done, n + 1)
                    nc.vector.reciprocal(rstd[:], sd[:]).then_inc(rstd_done, 1)
                    dve.wait_ge(rstd_done, n + 1)
                    for t in range(TT):
                        nc.vector.tensor_scalar(xn[:, t, :], buf[:, t, :], mean_var[:, t, 0:1], rstd[:, t:t + 1],
                                                ALU.subtract, ALU.mult).then_inc(xn_done, 1)

                def split_xn(n):
                    for e in range(ET):
                        dve.wait_ge(xhi_done, n * ET + e + 1)
                        nc.vector.tensor_tensor(a_lo[:, e, :], xf[:, e, 1:BLK + 1], a_hi[:, e, :].bitcast(F32),
                                                ALU.subtract).then_inc(xlo_done, 1)

                nc.vector.memset(xf[:, :, 0], 0.0).then_inc(col_zero, 1)
                moments(xb[0], 0, 16, 0)
                normalise(xb[0], 0)
                split_w(0)
                split_xn(0)
                for n in range(1, 6):
                    split_w(n)
                dve.wait_ge(small_ld, 48)
                dve.wait_ge(col_zero, 1)
                with dve.Fori(0, B) as i:
                    for blk in range(NB):
                        n = i * NB + blk
                        tile0 = i * (NB * NT) + blk * NT

                        def split_tile(m):
                            c = blk * 2 * G + m
                            dve.wait_ge(st_hi_done, i * (NB * 2 * G) + c + 1)
                            nc.vector.tensor_tensor(st_lo[c % NS][:], ring[(blk * NT + m) % RING][:],
                                                    st_hi[c % NS][:].bitcast(F32), ALU.subtract).then_inc(qk_done, 1)

                        def mixed(which):
                            dve.wait_ge(step_done, n + 1)
                            for e in range(ET):
                                nc.vector.scalar_tensor_tensor(
                                    out=mix[:, e, :], in0=xn[:, e, :], scalar=mus[:, which, e:e + 1],
                                    in1=xf[:, e, 0:BLK], op0=ALU.mult, op1=ALU.add).then_inc(mix_done, 1)

                        def mix_lo(which, dst, hi):
                            dve.wait_ge(mhi_done, n * 2 + which + 1)
                            nc.vector.tensor_tensor(dst[:], mix[:], hi[:].bitcast(F32), ALU.subtract)\
                                .then_inc(mlo_done, 1)

                        split_tile(0)
                        dve.wait_ge(xf_done, (n + 1) * ET)
                        nc.vector.tensor_tensor(xn[:], xf[:, :, 1:BLK + 1], xf[:, :, 0:BLK], ALU.subtract)\
                            .then_inc(step_done, 1)
                        split_tile(1)
                        if blk == 0:
                            dve.wait_ge(mlo_done, n * 2 + FIRST)
                        mixed(0)
                        split_tile(2)
                        split_tile(3)
                        mix_lo(0, b_lo, b_hi)
                        split_tile(4)
                        dve.wait_ge(mlo_done, n * 2 + 1 + FIRST)
                        mixed(1)
                        split_tile(5)
                        dve.wait_ge(mix_done, (n * 2 + 2) * ET)
                        if blk < NB - 1:
                            nc.vector.tensor_copy(xf[:, :, 0:1], xf[:, :, BLK:BLK + 1]).then_inc(col_zero, 1)
                        else:
                            nc.vector.memset(xf[:, :, 0:1], 0.0).then_inc(col_zero, 1)
                        s = (blk + 1) % 2
                        moments(xb[s], s, i * (NB // 2 * 16) + 16 * ((blk + 1) // 2 + 1), n + 1)
                        split_tile(6)
                        split_tile(7)
                        normalise(xb[s], n + 1)
                        mix_lo(1, a_lo, a_hi)

                        def to_gate(t):
                            dve.wait_ge(tanh_done, n * TT + t + 1 + FIRST)
                            nc.vector.tensor_scalar(gate[:, t, :], gate[:, t, :], 0.5, 0.5, ALU.mult, ALU.add)\
                                .then_inc(gate_done, 1)

                        def key(t):
                            dve.wait_ge(relu_done, n * TT + t + 1 + FIRST)
                            nc.vector.tensor_tensor(relu[t % 2][:], relu[t % 2][:], relu[t % 2][:], ALU.mult)\
                                .then_inc(sq_done, 1)

                        def key_lo(t):
                            dve.wait_ge(chi_done, n * TT + t + 1)
                            nc.vector.tensor_tensor(b_lo[:, t, :], relu[t % 2][:], b_hi[:, t, :].bitcast(F32),
                                                    ALU.subtract).then_inc(clo_done, 1)

                        to_gate(0)
                        to_gate(1)
                        to_gate(2)
                        to_gate(3)
                        key(0)
                        key(1)
                        key_lo(0)
                        key(2)
                        key_lo(1)
                        key(3)
                        key_lo(2)
                        key_lo(3)
                        split_xn(n + 1)
                        dve.wait_ge(gate_done, (n + 1) * TT)
                        for t in range(TT):
                            c = blk * TT + t
                            dve.wait_ge(tile_done, tile0 + F0 + t + 1)
                            dve.wait_ge(part_stored[c % 2], i * (NB * TT // 2 * 16) + 16 * (c // 2) + DMA_FIRST)
                            nc.vector.tensor_tensor(f_out[c % 2][:], ring[(blk * NT + F0 + t) % RING][:],
                                                    gate[:, t, :], ALU.mult).then_inc(f_done, 1)

            @block.tensor
            def _(pe):
                def transposes(n, tiles, first=False):
                    pe.wait_ge(xn_done, (n + 1) * TT)
                    for e in tiles:
                        if e >= 2:
                            pe.wait_ge(xf_done, n * ET + e - 1)
                        elif e == 0 and not first:
                            pe.wait_ge(xf_done, n * ET)
                        for t in range(TT):
                            last = nc.tensor.transpose(tps[e % 2][:, t * P:(t + 1) * P], xn[:, t, e * P:(e + 1) * P],
                                                       ident[:])
                        last.then_inc(t_done, 1)

                def product(n0, m, pairs, operand=None):
                    wait_ring(pe, n0, m)
                    out = ring[(n0[1] * NT + m) % RING]
                    for k, (lhs, rhs) in enumerate(pairs):
                        if operand and k % 3 == 0:
                            pe.wait_ge(operand[0], operand[1] + k // 3 + 1)
                        last = nc.tensor.matmul(out[:], lhs, rhs, start=(k == 0), stop=(k == len(pairs) - 1))
                    last.then_inc(tile_done, 1)

                def channels_out(a, w, cols):
                    return [(wx[:, e, cols], ax[:, e, :]) for e in range(ET)
                            for wx, ax in ((w_hi[w], a[0]), (w_hi[w], a[1]), (w_lo[w], a[0]))]

                def tokens_out(a, w, cols):
                    return [(ax[:, e, cols], wx[:, e, :]) for e in range(ET)
                            for ax, wx in ((a[0], w_hi[w]), (a[0], w_lo[w]), (a[1], w_hi[w]))]

                a, b = (a_hi, a_lo), (b_hi, b_lo)
                tile = [slice(t * P, (t + 1) * P) for t in range(4)]
                pe.wait_ge(ident_set, 1)
                transposes(0, range(ET), first=True)
                with pe.Fori(0, B) as i:
                    for blk in range(NB):
                        n = i * NB + blk
                        n0 = (i, blk)
                        pe.wait_ge(w_split, 1)
                        for g in range(G):
                            product(n0, Q0 + g, channels_out(a, 0, tile[g]), (xlo_done, n * ET) if g == 0 else None)
                        pe.wait_ge(w_split, 2)
                        for g in range(G):
                            product(n0, K0 + g, channels_out(a, 1, tile[g]))
                        pe.wait_ge(w_split, 3)
                        for t in range(TT):
                            product(n0, V0 + t, tokens_out(a, 2, tile[t]))
                        pe.wait_ge(w_split, 6)
                        pe.wait_ge(mlo_done, n * 2 + 1 + FIRST)
                        for t in range(TT):
                            product(n0, R0 + t, tokens_out(b, 3, tile[t]))
                        pe.wait_ge(mlo_done, n * 2 + 2 + FIRST)
                        for t in range(TT):
                            product(n0, C0 + t, channels_out(a, 4, tile[t]))
                        transposes(n + 1, range(2))
                        for t in range(TT):
                            product(n0, F0 + t, tokens_out(b, 5, tile[t]),
                                    (clo_done, n * TT + FIRST) if t == 0 else None)
                            if t == 0:
                                transposes(n + 1, range(2, ET))


def attention(nc, q_hi, q_lo, k_hi, k_lo, v_all, ctx_t):
    NG = B * G
    KT = T // P
    STEPS = [TT * (j + 1) for j in range(NB)]
    S0 = [sum(STEPS[:j]) for j in range(NB)]
    NSTEP = sum(STEPS)
    STEP_PAIRS = NSTEP // 2
    NPR = 5
    NX = 3
    ENTRY = []
    for j in range(NB):
        chunks = [(j, h, r, c) for h in range(HG) for r in range(TT) for c in range(j + 1)]
        ENTRY += chunks[:2 * NX] + ([(j - 1,)] if j else []) + chunks[2 * NX:]
    ENTRY.append((NB - 1,))
    NENT = len(ENTRY)
    TAKEN = [sum(len(x) > 1 for x in ENTRY[:e + 1]) for e in range(NENT)]
    NTAKE = TAKEN[-1]
    AHEAD = 84
    ROWS_AHEAD = sum(len(x) == 1 for x in ENTRY[:AHEAD])

    def share_out():
        LATENCY = 250
        pieces = []
        for n in range(NSTEP):
            j = max(j for j in range(NB) if S0[j] <= n)
            r = n - S0[j] - j * TT
            w = BLK - max(r, 0) * P
            qk = (max(w, 2 * P) + (P if r >= 0 else 0)) / 2.4 + 50
            invert = 870 if 1 <= n - S0[j] <= TT else 0
            pieces += [(qk, invert), (qk, 0), (4 * w / 2.4 + 70, 0), (qk, 0), (qk, 0),
                       (4 * w / 2.4 + 70 if n % 2 else 0, 0)]
        entries = ENTRY[AHEAD:] + ENTRY[:AHEAD]

        def cost(x):
            return 200 if len(x) == 1 else 30 + (BLK if x[3] < x[0] else (x[2] + 1) * P) / 0.96

        def place(rate):
            out, begun, now, dve, spare, freed, neg = [], 0, 0, 0, 0, [0] * NX, 0
            for own, invert in pieces:
                now += own
                dve = max(dve, now) + invert if invert else dve
                spare += own * rate - invert
                first = begun
                while begun < NENT and spare >= 0:
                    x = entries[begun]
                    if now < max(freed[-NX] + LATENCY / 2, neg + LATENCY / 2 if len(x) == 1 else 0):
                        break
                    spare -= cost(x)
                    mm = P / 2.4 if len(x) == 1 else max(BLK if x[3] < x[0] else (x[2] + 1) * P, 2 * P) / 2.4
                    now += mm
                    dve = max(dve, now + LATENCY) + cost(x)
                    freed.append(dve)
                    if x[1:] == (HG - 1, TT - 1, x[0]):
                        neg = dve = dve + 330
                    begun += 1
                out.append((AHEAD + first, AHEAD + begun))
            return out

        rate, out = 0.5, place(0.5)
        while out[-1][1] < AHEAD + NENT:
            rate *= 1.01
            out = place(rate)
        return out

    SHARE = share_out()
    NPIECE = len(SHARE) // NSTEP

    def step(x):
        over, n = divmod(x, NSTEP)
        j = max(j for j in range(NB) if S0[j] <= n)
        return over, j, n - S0[j], n

    def unit_ended(x, last):
        over, j, kt, n = step(x)
        return over * NB + j if x >= 0 and kt == STEPS[j] - 1 and not (last and over == 2) else None

    PEEL = 6
    GROUP_PAIRS = NG // 2
    PAIR_STEPS = 2 * NSTEP

    BEFORE = 40
    PEELED = SHARE[PEEL * NPIECE - 1][1] - BEFORE

    def entries_of(x, last, peeled=False):
        if peeled:
            cuts = [BEFORE + PEELED * k // (PEEL * NPIECE) for k in range(x * NPIECE, (x + 1) * NPIECE + 1)]
            return [[(0, e) for e in range(a, b)] for a, b in zip(cuts, cuts[1:])]
        over, j, kt, n = step(x)
        pieces = [[(over + p // NENT, p % NENT) for p in range(*SHARE[n * NPIECE + k])] for k in range(NPIECE)]
        return [[x for x in piece if not (last and x[0] >= 2)] for piece in pieces]

    def bank(place, period):
        return place % period % NX

    def bank_before(place, period):
        at = place % period
        return place - NX if at >= NX else place - at - 1 - (period - 1 - at) % NX

    with ExitStack() as ctx:
        def sb(name, shape, dt=F32):
            return ctx.enter_context(nc.sbuf_tensor(name, shape, dt))

        def sem(name):
            return ctx.enter_context(nc.semaphore(name))

        qs = [sb(f"q_stack{s}", [P, HG, T], F32R) for s in range(2)]
        ks = [sb(f"k_stack{s}", [P, HG, T], F32R) for s in range(2)]
        vs = [sb(f"v_group{s}", [P, KT, P]) for s in range(2)]
        pr = [sb(f"probs{s}", [P, HG, BLK]) for s in range(NPR)]
        o_sb = [sb(f"o_sb{s}", [P, BLK]) for s in range(2)]
        s_sb = [sb(f"s_sb{s}", [P, BLK]) for s in range(2)]
        o_n = [sb(f"o_norm{s}", [P, BLK]) for s in range(2)]
        tri = sb("tri", [P, BLK])
        junk = [sb(f"junk{s}", [P, BLK]) for s in range(NX)]
        m_part = sb("m_part", [P, HG * TT, NB])
        m_neg = [sb(f"m_neg{s}", [P, HG * TT]) for s in range(2)]
        m_row = [sb(f"m_row{s}", [HG * TT, P], F32R) for s in range(2)]
        ident = sb("ident2", [P, P])
        ident_b = sb("ident_b", [P, P], BF16)
        tri_b = sb("tri_b", [P, P], BF16)
        ones = sb("ones", [P, HD])
        sT = [ctx.enter_context(nc.psum_tensor(f"scores_t{h}", [P, BLK], F32)) for h in range(NX)]
        mx = [ctx.enter_context(nc.psum_tensor(f"scores{s}", [P, BLK], F32)) for s in range(NX)]
        o_ps = ctx.enter_context(nc.psum_tensor("o_ps", [P, BLK], F32))
        s_ps = ctx.enter_context(nc.psum_tensor("s_ps", [P, BLK], F32))

        q_ld = [[sem(f"q_loaded{s}{j}") for j in range(NB)] for s in range(2)]
        kv_ld = [[sem(f"kv_loaded{s}{j}") for j in range(NB)] for s in range(2)]
        m_ld = [sem(f"m_loaded{j}") for j in range(NB)]
        o_st = [sem(f"o_stored{s}") for s in range(2)]
        cst0 = sem("const_filled")
        cst = sem("const_ready")
        one_rows = sem("one_rows_ready")
        mm_done = sem("chunk_done")
        mx_freed = sem("chunk_taken")
        neg_done = sem("m_neg_ready")
        row_done = sem("m_row_ready")
        qk_done = sem("scores_t_done")
        ex_done = sem("probs_done")
        pv_done = sem("pv_done")
        pair_done = sem("pair_added")
        sm_done = sem("sum_done")
        o_cp = sem("o_copied")
        s_cp = sem("s_copied")
        rc_done = sem("recip_done")
        on_done = sem("o_norm_done")

        with nc.Block() as block:
            def load_q(sp, g, par, j):
                src = [a[bass.ds(g * P, P), j * BLK:(j + 1) * BLK].rearrange("(h d) t -> d h t", h=HG)
                       for a in (q_hi, q_hi, q_lo)]
                for c in range(3):
                    sp.dma_start(qs[par][c * HD:(c + 1) * HD, :, j * BLK:(j + 1) * BLK].bitcast(F32), src[c]
                                 ).then_inc(q_ld[par][j], 16)

            def load_kv(sp, g, par, j):
                src = [a[bass.ds(g * P, P), j * BLK:(j + 1) * BLK].rearrange("(h d) t -> d h t", h=HG)
                       for a in (k_hi, k_lo, k_hi)]
                for c in range(3):
                    sp.dma_start(ks[par][c * HD:(c + 1) * HD, :, j * BLK:(j + 1) * BLK].bitcast(F32), src[c]
                                 ).then_inc(kv_ld[par][j], 16)
                sp.dma_start(vs[par][:, j * TT:(j + 1) * TT, :],
                             v_all[bass.ds(g * T + j * BLK, BLK), :].rearrange("(t p) c -> p t c", p=P)
                             ).then_inc(kv_ld[par][j], 16)

            def store_m(sp, mg, par, j):
                u = j % 2
                sp.wait_ge(row_done, mg * NB + j + 1)
                for h in range(HG):
                    sp.dma_start(qs[par][QK_ROWS:QK_ROWS + 1, h, j * BLK:(j + 1) * BLK].bitcast(F32),
                                 m_row[u][h * TT:(h + 1) * TT, :].bitcast(F32)).then_inc(m_ld[j], 16)

            @block.sync
            def _(sp):
                start_counters(sp, [on_done], o_st)
                for j in range(NB):
                    load_q(sp, 0, 0, j)
                    load_kv(sp, 0, 0, j)
                for j in range(ROWS_AHEAD):
                    store_m(sp, 0, 0, j)
                for j in range(NB):
                    load_q(sp, 1, 1, j)
                    load_kv(sp, 1, 1, j)

                def store_o(g0, u):
                    par, j = divmod(u, NB)
                    sp.wait_ge(on_done, g0 * NB + u + 1 + FIRST)
                    sp.dma_start(ctx_t[bass.ds((g0 + par) * P, P), j * BLK:(j + 1) * BLK], o_n[u % 2][:]
                                 ).then_inc(o_st[u % 2], 16)

                def body(g0, last):
                    for par in range(2):
                        g = g0 + par
                        for j in range(NB):
                            u = par * NB + j
                            if not last:
                                if j == NB - 1:
                                    for c in range(NB - 1):
                                        sp.wait_ge(pv_done, g * NSTEP + S0[j] + (c + 1) * TT)
                                        load_kv(sp, g + 2, par, c)
                            if u >= 1:
                                store_o(g0, u - 1)
                            if j < NB - ROWS_AHEAD:
                                store_m(sp, g, par, ROWS_AHEAD + j)
                            elif not (last and par == 1):
                                store_m(sp, g + 1, 1 - par, j - (NB - ROWS_AHEAD))
                            if not last:
                                sp.wait_ge(qk_done, g * (NSTEP * HG) + (S0[j] + STEPS[j]) * HG)
                                load_q(sp, g + 2, par, j)
                        if not last:
                            sp.wait_ge(pv_done, (g + 1) * NSTEP)
                            load_kv(sp, g + 2, par, NB - 1)
                    store_o(g0, 2 * NB - 1)

                with sp.Fori(0, GROUP_PAIRS - 1) as i:
                    body(2 * i, False)
                body(NG - 2, True)
                for s in range(2):
                    sp.wait_ge(o_st[s], NG * NB // 2 * 16 + DMA_FIRST)

            @block.gpsimd
            def _(pool):
                nc.gpsimd.memset(ones[:], 1.0).then_inc(cst, 1)
                nc.gpsimd.memset(ident[:], 1.0).then_inc(cst0, 1)
                nc.gpsimd.memset(tri[:], 0.0).then_inc(cst0, 1)
                nc.gpsimd.memset(ident_b[:], 1.0).then_inc(cst0, 1)
                nc.gpsimd.memset(tri_b[:], 0.0).then_inc(cst0, 1)
                pool.wait_ge(cst0, 4)
                nc.gpsimd.affine_select(out=ident_b[:], in_=ident_b[:], compare_op=ALU.is_equal, fill=0.0, base=0,
                                        pattern=[[-1, P]], channel_multiplier=1).then_inc(cst, 1)
                nc.gpsimd.affine_select(out=tri_b[:], in_=tri_b[:], compare_op=ALU.is_ge, fill=MASKED, base=0,
                                        pattern=[[1, P]], channel_multiplier=-1).then_inc(cst, 1)
                nc.gpsimd.affine_select(out=ident[:], in_=ident[:], compare_op=ALU.is_equal, fill=0.0, base=0,
                                        pattern=[[-1, P]], channel_multiplier=1).then_inc(cst, 1)
                nc.gpsimd.affine_select(out=tri[:, BLK - P:BLK], in_=tri[:, BLK - P:BLK], compare_op=ALU.is_ge,
                                        fill=MASKED, base=0, pattern=[[-1, P]], channel_multiplier=1).then_inc(cst, 1)
                pool.wait_ge(cst, 5)
                for s in range(2):
                    nc.gpsimd.memset(ks[s][QK_ROWS:QK_ROWS + 1, :, :].bitcast(F32), 1.0).then_inc(one_rows, 1)
                pool.wait_ge(one_rows, 2)

                def at(g0, x, last):
                    over, j, kt, n = step(x)
                    g = g0 + over
                    if n % 2 == 1 and not (last and over == 2):
                        col = max(kt - j * TT, 0) * P
                        pool.wait_ge(ex_done, (g * NSTEP + n + 1) * HG)
                        pool.wait_ge(pv_done, g * NSTEP + n)
                        even, odd = pr[(x - 1) % NPR], pr[x % NPR]
                        nc.gpsimd.tensor_tensor(even[:, :, col:], even[:, :, col:], odd[:, :, col:], ALU.add)\
                            .then_inc(pair_done, 1)
                    u = unit_ended(x - 6, last)
                    if u is not None:
                        pool.wait_ge(rc_done, (g0 * NB + u + 1) * TT)
                        pool.wait_ge(o_st[u % 2], (g0 * NB + u - u % 2) * 8 + DMA_FIRST)
                        nc.gpsimd.tensor_tensor(o_n[u % 2][:], o_sb[u % 2][:], s_sb[u % 2][:], ALU.mult)\
                            .then_inc(on_done, 1)

                for x in range(PEEL):
                    at(0, x, False)
                with pool.Fori(0, GROUP_PAIRS - 1) as i:
                    for x in range(PEEL, PAIR_STEPS + PEEL):
                        at(2 * i, x, False)
                for x in range(PEEL, PAIR_STEPS + PEEL):
                    at(NG - 2, x, True)

            @block.scalar
            def _(act):
                def exponentials(g0, x, heads):
                    over, j, kt, n = step(x)
                    col = max(kt - j * TT, 0) * P
                    for h in heads:
                        act.wait_ge(qk_done, (g0 * NSTEP + x) * HG + h + 1)
                        nc.scalar.activation(pr[x % NPR][:, h, col:], sT[bank(x * HG + h, PAIR_STEPS * HG)][:, col:],
                                             ACT.Exp, scale=SCALE).then_inc(ex_done, 1)

                def at(g0, x, last):
                    live = not (last and x >= PAIR_STEPS)
                    if live:
                        if x >= NPR:
                            act.wait_ge(sm_done, g0 * STEP_PAIRS + (x - NPR) // 2 + 1)
                        exponentials(g0, x, (0, 1))
                    u = unit_ended(x - 1, last)
                    if u is not None:
                        act.wait_ge(on_done, g0 * NB + max(u - 1, 0) + FIRST)
                        act.wait_ge(pv_done, g0 * NSTEP + x)
                        nc.scalar.activation(o_sb[u % 2][:], o_ps[:], ACT.Copy).then_inc(o_cp, 1)
                    if live:
                        exponentials(g0, x, (2, 3))
                    u = unit_ended(x - 2, last)
                    if u is not None:
                        act.wait_ge(sm_done, g0 * STEP_PAIRS + (x - 1) // 2)
                        nc.scalar.activation(s_sb[u % 2][:], s_ps[:], ACT.Copy).then_inc(s_cp, 1)

                for x in range(PEEL):
                    at(0, x, False)
                with act.Fori(0, GROUP_PAIRS - 1) as i:
                    for x in range(PEEL, PAIR_STEPS + PEEL):
                        at(2 * i, x, False)
                for x in range(PEEL, PAIR_STEPS + PEEL):
                    at(NG - 2, x, True)

            @block.vector
            def _(dve):
                dve.wait_ge(cst, 5)

                def take(mg0, over, e, first=False):
                    mg = mg0 + over
                    s = bank(over * NENT + e - AHEAD, 2 * NENT)
                    dve.wait_ge(mm_done, mg * NENT + e + 1)
                    if len(ENTRY[e]) == 1:
                        j, = ENTRY[e]
                        if j >= 2:
                            dve.wait_ge(m_ld[j - 2], (mg + 1) * (HG * 16))
                        elif not first:
                            dve.wait_ge(m_ld[j + 2], mg * (HG * 16))
                        nc.vector.tensor_copy(m_row[j % 2][:], mx[s][0:HG * TT, 0:P]).then_inc(row_done, 1)
                        return
                    j, h, r, c = ENTRY[e]
                    if (h, r, c) == (0, 0, 0) and not (first and j == 0):
                        dve.wait_ge(neg_done, mg * NB + j)
                    dst = m_part[:, h * TT + r, c:c + 1]
                    if c < j:
                        nc.vector.tensor_reduce(dst, mx[s][:], AX_X, ALU.max).then_inc(mx_freed, 1)
                    else:
                        w = (r + 1) * P
                        dve.nop(nofuse=True)
                        nc.vector.tensor_tensor_reduce(
                            out=junk[s][:, 0:w], in0=mx[s][:, 0:w], in1=tri[:, BLK - w:BLK], scale=1.0,
                            scalar=MASKED, op0=ALU.add, op1=ALU.max, accum_out=dst).then_inc(mx_freed, 1)
                    if (h, r, c) == (HG - 1, TT - 1, j):
                        dve.wait_ge(mx_freed, mg * NTAKE + TAKEN[e])
                        nc.vector.tensor_reduce(m_neg[j % 2][:], m_part[:, :, 0:j + 1], AX_X, ALU.max,
                                                negate=True).then_inc(neg_done, 1)

                for e in range(BEFORE):
                    take(0, 0, e, first=True)

                def at(g0, x, last, peeled=False):
                    for piece in entries_of(x, last, peeled):
                        for over, e in piece:
                            take(g0, over, e, first=peeled)
                    for piece in range(TT):
                        u = unit_ended(x - 2 - piece, last)
                        if u is not None:
                            dve.wait_ge(s_cp, g0 * NB + u + 1)
                            sums = s_sb[u % 2][:, piece * P:(piece + 1) * P]
                            nc.vector.reciprocal(sums, sums).then_inc(rc_done, 1)

                for x in range(PEEL):
                    at(0, x, False, peeled=True)
                with dve.Fori(0, GROUP_PAIRS - 1) as i:
                    for x in range(PEEL, PAIR_STEPS + PEEL):
                        at(2 * i, x, False)
                for x in range(PEEL, PAIR_STEPS + PEEL):
                    at(NG - 2, x, True)

            @block.tensor
            def _(pe):
                pe.wait_ge(cst, 5)

                def entry(i, over, e, first=False):
                    mpar, mg = over % 2, 2 * i + over
                    place = over * NENT + e - AHEAD
                    dst = mx[bank(place, 2 * NENT)]
                    if not first or e >= NX:
                        og, oe = divmod(bank_before(place, 2 * NENT) + AHEAD, NENT)
                        if len(ENTRY[oe]) == 1:
                            pe.wait_ge(row_done, (2 * i + og) * NB + ENTRY[oe][0] + 1)
                        else:
                            pe.wait_ge(mx_freed, (2 * i + og) * NTAKE + TAKEN[oe])
                    if len(ENTRY[e]) == 1:
                        j, = ENTRY[e]
                        pe.wait_ge(neg_done, mg * NB + j + 1)
                        nc.tensor.transpose(dst[0:HG * TT, 0:P], m_neg[j % 2][:], ident[:]).then_inc(mm_done, 1)
                        return
                    j, h, r, c = ENTRY[e]
                    if (h, r, c) == (0, 0, 0):
                        pe.wait_ge(kv_ld[mpar][j], (i + over // 2 + 1) * 64)
                        pe.wait_ge(q_ld[mpar][j], (i + over // 2 + 1) * 48)
                    w = BLK if c < j else max((r + 1) * P, 2 * P)
                    q0 = j * BLK + r * P
                    nc.tensor.matmul(dst[:, 0:w], qs[mpar][0:QK_ROWS, h, q0:q0 + P],
                                     ks[mpar][0:QK_ROWS, h, c * BLK:c * BLK + w], start=True, stop=True)\
                        .then_inc(mm_done, 1)

                def scores(g0, x, h):
                    over, j, kt, n = step(x)
                    par = over % 2
                    q = x * HG + h
                    dst = sT[bank(q, PAIR_STEPS * HG)]
                    if kt == 0 and h == 0:
                        pe.wait_ge(m_ld[j], (g0 + over + 1) * (HG * 16))
                    if q >= NX:
                        pe.wait_ge(ex_done, g0 * (NSTEP * HG) + bank_before(q, PAIR_STEPS * HG) + 1)
                    col = min(max(kt - j * TT, 0) * P, BLK - 2 * P)
                    last = nc.tensor.matmul(dst[:, col:], ks[par][0:QK_ROWS + 1, h, kt * P:(kt + 1) * P],
                                            qs[par][0:QK_ROWS + 1, h, j * BLK + col:(j + 1) * BLK],
                                            start=True, stop=True)
                    if kt >= j * TT:
                        d = (kt - j * TT) * P
                        last = nc.tensor.matmul(dst[:, d:d + P], ident_b[:], tri_b[:], start=False, stop=True,
                                                skip_group_check=True)
                    last.then_inc(qk_done, 1)

                def side_by_side(dst, x, lhs):
                    over, j, kt, n = step(x)
                    col = max(kt - j * TT, 0) * P
                    for h in range(HG):
                        last = nc.tensor.matmul(dst[h * HD:(h + 1) * HD, col:], lhs[h], pr[x % NPR][:, h, col:],
                                                start=(kt == 0), stop=(kt >= STEPS[j] - (1 if dst is o_ps else 2)))
                    return last

                def weigh(g0, x):
                    over, j, kt, n = step(x)
                    pe.wait_ge(ex_done, (g0 * NSTEP + x + 1) * HG)
                    if kt == 0 and x > 0:
                        pe.wait_ge(o_cp, (g0 + over) * NB + j)
                    side_by_side(o_ps, x, [vs[over % 2][:, kt, h * HD:(h + 1) * HD] for h in range(HG)])\
                        .then_inc(pv_done, 1)

                def total(g0, x):
                    over, j, kt, n = step(x)
                    if kt == 0 and x > 0:
                        pe.wait_ge(s_cp, (g0 + over) * NB + j)
                    pe.wait_ge(pair_done, g0 * STEP_PAIRS + x // 2 + 1)
                    side_by_side(s_ps, x, [ones[:]] * HG).then_inc(sm_done, 1)

                def at(i, g0, x, last, peeled=False):
                    entries = entries_of(x, last, peeled)

                    def begin(piece):
                        for over, e in entries[piece]:
                            entry(i, over, e, first=peeled)

                    live = not (last and x >= PAIR_STEPS)
                    if live:
                        scores(g0, x, 0)
                        begin(0)
                        scores(g0, x, 1)
                        begin(1)
                    if x >= 1 and not (last and x > PAIR_STEPS):
                        weigh(g0, x - 1)
                    if live:
                        begin(2)
                        scores(g0, x, 2)
                        begin(3)
                        scores(g0, x, 3)
                        begin(4)
                    if x >= 3 and x % 2 == 1 and not (last and x - 3 >= PAIR_STEPS):
                        total(g0, x - 3)
                    if live:
                        begin(5)

                for e in range(BEFORE):
                    entry(0, 0, e, first=True)
                pe.wait_ge(one_rows, 2)
                for x in range(PEEL):
                    at(0, 0, x, False, peeled=True)
                with pe.Fori(0, GROUP_PAIRS - 1) as i:
                    for x in range(PEEL, PAIR_STEPS + PEEL):
                        at(i, 2 * i, x, False)
                for x in range(PEEL, PAIR_STEPS + PEEL):
                    at(GROUP_PAIRS - 1, NG - 2, x, True)


def project_out(nc, ctx_t, w_o, part, out):
    NBLK = B * NB
    with ExitStack() as ctx:
        def sb(name, shape, dt=F32):
            return ctx.enter_context(nc.sbuf_tensor(name, shape, dt))

        def sem(name):
            return ctx.enter_context(nc.semaphore(name))

        w_raw = sb("wo_raw", [P, ET, D])
        w_hi = sb("wo_hi", [P, ET, D], F32R)
        w_lo = sb("wo_lo", [P, ET, D], F32R)
        c_raw = [sb(f"ctx{s}", [P, ET, BLK]) for s in range(2)]
        c_hi = [sb(f"ctx_hi{s}", [P, ET, BLK], F32R) for s in range(2)]
        c_lo = [sb(f"ctx_lo{s}", [P, ET, BLK], F32R) for s in range(2)]
        res = [sb(f"res{s}", [P, TT, D]) for s in range(2)]
        ps = [ctx.enter_context(nc.psum_tensor(f"out_ps{s}", [P, D], F32)) for s in range(2 * TT)]
        w_ld = [sem(f"wo_loaded{e}") for e in range(ET)]
        whi = sem("wo_hi_ready")
        wlo = sem("wo_lo_ready")
        c_ld = [[sem(f"ctx_loaded{s}{e}") for e in range(ET)] for s in range(2)]
        r_ld = [sem(f"res_loaded{s}") for s in range(2)]
        chi = sem("ctx_hi_ready")
        clo = sem("ctx_lo_ready")
        done = sem("out_tile_done")
        added = sem("out_added")
        stored = [sem(f"out_stored{s}") for s in range(2)]
        TWO_LATE = [(clo, ET), (done, TT), (added, TT)]

        with nc.Block() as block:
            @block.sync
            def _(sp):
                for counter, of_block in TWO_LATE:
                    sp.sem_inc(counter, 2 * of_block)
                start_counters(sp, [], stored)
                for e in range(ET):
                    sp.dma_start(w_raw[:, e, :], w_o[e * P:(e + 1) * P, :]).then_inc(w_ld[e], 16)
                with sp.Fori(0, B) as i:
                    for j in range(NB):
                        s = j % 2
                        n = i * NB + j
                        half = i * (NB // 2) + j // 2
                        sp.wait_ge(clo, (n + 1) * ET)
                        for e in range(ET):
                            sp.dma_start(c_raw[s][:, e, :],
                                         ctx_t[bass.ds(i * (G * P) + e * P, P), j * BLK:(j + 1) * BLK]
                                         ).then_inc(c_ld[s][e], 16)
                        sp.wait_ge(stored[s], half * 16 + DMA_FIRST)
                        sp.dma_start(res[s][:], part[bass.ds(i * T + j * BLK, BLK), :]
                                     .rearrange("(t p) d -> p t d", p=P)).then_inc(r_ld[s], 16)
                for s in range(2):
                    sp.wait_ge(stored[s], NBLK // 2 * 16 + DMA_FIRST)

            @block.scalar
            def _(act):
                for e in range(ET):
                    act.wait_ge(w_ld[e], 16)
                    nc.scalar.activation(w_hi[:, e, :], w_raw[:, e, :], ACT.Copy).then_inc(whi, 1)

                def split(i, j):
                    s = j % 2
                    n = i * NB + j
                    half = i * (NB // 2) + j // 2
                    act.wait_ge(done, (n + 1) * TT)
                    for e in range(ET):
                        act.wait_ge(c_ld[s][e], half * 16 + 16)
                        nc.scalar.activation(c_hi[s][:, e, :], c_raw[s][:, e, :], ACT.Copy).then_inc(chi, 1)

                def store(i, j):
                    act.wait_ge(added, (i * NB + j + 1) * TT + 2 * TT)
                    act.dma_start(out[bass.ds(i * T + j * BLK, BLK), :].rearrange("(t p) d -> p t d", p=P),
                                  res[j % 2][:]).then_inc(stored[j % 2], 16)

                split(0, 0)
                with act.Fori(0, B - 1) as i:
                    for j in range(NB):
                        split(i, j + 1)
                        store(i, j)
                for j in range(NB):
                    if j < NB - 1:
                        split(B - 1, j + 1)
                    store(B - 1, j)

            @block.gpsimd
            def _(pool):
                with pool.Fori(0, B) as i:
                    for j in range(NB):
                        s = j % 2
                        n = i * NB + j
                        for e in range(ET):
                            pool.wait_ge(chi, n * ET + e + 1)
                            nc.gpsimd.tensor_tensor(c_lo[s][:, e, :], c_raw[s][:, e, :],
                                                    c_hi[s][:, e, :].bitcast(F32), ALU.subtract).then_inc(clo, 1)

            @block.vector
            def _(dve):
                for e in range(ET):
                    dve.wait_ge(whi, e + 1)
                    nc.vector.tensor_tensor(w_lo[:, e, :], w_raw[:, e, :], w_hi[:, e, :].bitcast(F32),
                                            ALU.subtract).then_inc(wlo, 1)

                with dve.Fori(0, B) as i:
                    for j in range(NB):
                        s = j % 2
                        n = i * NB + j
                        half = i * (NB // 2) + j // 2
                        dve.wait_ge(r_ld[s], half * 16 + 16)
                        for t in range(TT):
                            dve.wait_ge(done, n * TT + t + 1 + 2 * TT)
                            nc.vector.tensor_tensor(res[s][:, t, :], ps[s * TT + t][:], res[s][:, t, :], ALU.add)\
                                .then_inc(added, 1)

            @block.tensor
            def _(pe):
                pe.wait_ge(wlo, ET)
                with pe.Fori(0, B) as i:
                    for j in range(NB):
                        s = j % 2
                        n = i * NB + j
                        pe.wait_ge(added, (n + 1) * TT)
                        for e in range(ET):
                            pe.wait_ge(clo, n * ET + e + 1 + 2 * ET)
                            for t in range(TT):
                                for k, (cx, wx) in enumerate(((c_hi[s], w_hi), (c_hi[s], w_lo), (c_lo[s], w_hi))):
                                    last = nc.tensor.matmul(ps[s * TT + t][:], cx[:, e, t * P:(t + 1) * P], wx[:, e, :],
                                                            start=(e + k == 0), stop=(e == ET - 1 and k == 2))
                                if e == ET - 1:
                                    last.then_inc(done, 1)


def build_program(nc, x, w_t, w_o, b_o, mu_r, mu_k, out):
    def scratch(name, shape, dt=F32):
        return nc.dram_tensor(name, shape, dt, kind="Internal").ap()

    split = [scratch(n, [B * G * P, T]) for n in ("q_hi", "q_lo", "k_hi", "k_lo")]
    v_all = scratch("v_all", [B * G * T, P])
    part = scratch("part", [B * T, D])
    ctx_t = scratch("ctx_t", [B * G * P, T])
    project_and_ffn(nc, x, w_t, b_o, mu_r, mu_k, *split, v_all, part)
    attention(nc, *split, v_all, ctx_t)
    project_out(nc, ctx_t, w_o, part, out)


def kernel(**inputs):
    import numpy as _np
    import concourse.bacc as _bacc
    from concourse import mybir as _mybir
    from concourse.bass_utils import run_bass_kernel_spmd as _run

    nc = _bacc.Bacc("TRN2", target_bir_lowering=False, num_devices=1)
    nc.disable_value_cache = True
    a = {k: _np.asarray(v) for k, v in inputs.items()}
    laid = {
        "x": a["L0_attn_x"].reshape(B * T, D),
        "b_o": _np.broadcast_to(a["L0_attn_b_o"], (P, D)),
        "mu_r": a["L0_ffn_mu_r"].reshape(ET, P).T,
        "mu_k": a["L0_ffn_mu_k"].reshape(ET, P).T,
    }
    names = ["L0_attn_W_q", "L0_attn_W_k", "L0_attn_W_v", "L0_ffn_W_r", "L0_ffn_W_k", "L0_ffn_W_v", "L0_attn_W_o"]
    for n, name in enumerate(names):
        laid[f"w{n}"] = a[name].T
    laid = {k: _np.ascontiguousarray(v) for k, v in laid.items()}
    h = {k: nc.dram_tensor(f"in_{k}", v.shape, _mybir.dt.from_np(v.dtype), kind="ExternalInput").ap()
         for k, v in laid.items()}
    out = nc.dram_tensor("out_0", (B * T, D), _mybir.dt.float32, kind="ExternalOutput").ap()
    build_program(nc, h["x"], [h[f"w{n}"] for n in range(6)], h["w6"], h["b_o"], h["mu_r"], h["mu_k"], out)
    r = _run(nc, [{f"in_{k}": v for k, v in laid.items()}], core_ids=[0])
    return r.results[0]["out_0"].reshape(B, T, D)
```
